# Optimizing a Trainium2 kernel written in Bass

```python
import numpy as np
import jax
import jax.numpy as jnp

def _softmax(x, axis=-1):
    return jax.nn.softmax(x, axis=axis)

def _gelu(x):
    return jax.nn.gelu(x, approximate=True)

def _silu(x):
    return jax.nn.silu(x)

def _sigmoid(x):
    return jax.nn.sigmoid(x)

def _layernorm(x, axis=-1, eps=1e-05):
    m = jnp.mean(x, axis=axis, keepdims=True)
    v = jnp.var(x, axis=axis, keepdims=True)
    return (x - m) / jnp.sqrt(v + eps)

def _scatter_add(tgt, idx, src, axis=0):
    return tgt.at[idx].add(src)

def _segment_sum(src, seg, n):
    return jax.ops.segment_sum(src, seg, n)
kernel_name = 'mk_xattn_ffn_d1_seqx_r8_da6101'

def setup_inputs(seed: int=0):
    np.random.seed(seed)
    _w = jnp.asarray

    def _rec_inputs():
        import jax
        import jax.numpy as jnp
        _rk = jax.random.key(seed)
        x = 7.22e-05 + 1 * jax.random.normal(jax.random.fold_in(_rk, 1), (4, 256, 256), jnp.float32)
        _lenS = 256 - jax.random.randint(jax.random.fold_in(_rk, 7), (4,), 0, max(1, 256 // 4) + 1, jnp.int32)
        _lenS2 = 256 - jax.random.randint(jax.random.fold_in(_rk, 8), (4,), 0, max(1, 256 // 4) + 1, jnp.int32)
        _ctx_1024P = jax.random.normal(jax.random.fold_in(_rk, 11), (4, 16, 128), jnp.float32)
        _ctx_1024c = jax.random.dirichlet(jax.random.fold_in(_rk, 511), 0.3 * jnp.ones((16,), jnp.float32), (4, 256))
        _ctx_1024t = jnp.einsum('bsk,bkd->bsd', _ctx_1024c, _ctx_1024P)
        _ctx_1024t = _ctx_1024t * jax.lax.rsqrt(jnp.mean(jnp.square(_ctx_1024t)) + 1e-12) * 0.953939
        ctx_1024 = 2.81802e-05 + 1.00001 * (_ctx_1024t + 0.3 * jax.random.normal(jax.random.fold_in(_rk, 611), (4, 256, 128), jnp.float32))
        return (x, ctx_1024)
    x, ctx_1024 = _rec_inputs()

    def _L0_xattn_setup():
        import jax, jax.numpy as jnp
        import numpy as np
        key = jax.random.key(seed)
        ks = jax.random.split(key, 6)
        B, L, N, C, D = (8, 64, 256, 128, 128)
        return {'teacher_logits': jax.random.normal(ks[0], (B, L, N), dtype=jnp.float32), 'teacher_features': jax.random.normal(ks[1], (B, N, C), dtype=jnp.float32), 'Wq': jax.random.normal(ks[2], (D, C), dtype=jnp.float32) * (1.0 / np.sqrt(C)), 'bq': jnp.zeros((D,), dtype=jnp.float32), 'Wk': jax.random.normal(ks[3], (D, C), dtype=jnp.float32) * (1.0 / np.sqrt(C)), 'bk': jnp.zeros((D,), dtype=jnp.float32)}
    _L0_xattn_all = _L0_xattn_setup()
    _L0_xattn_in = {k: v for k, v in _L0_xattn_all.items() if k in ('Wq', 'bq', 'Wk', 'bk')}
    del _L0_xattn_all

    def _L0_ffn_setup():
        import math
        import jax, jax.numpy as jnp
        import numpy as np
        NUM_EXPERTS = 8
        HIDDEN = 256
        INTER = 1024
        CAP_FACTOR = 1.25
        MIN_CAP = 4
        B, S = (4, 256)

        def _capacity(num_tokens: int, num_experts: int) -> int:
            cap = math.floor(CAP_FACTOR * num_tokens / num_experts)
            cap += cap % 2
            return max(cap, MIN_CAP)
        key = jax.random.key(seed)
        k1, k2, k3, k4 = jax.random.split(key, 4)
        std_h = math.sqrt(0.1 / HIDDEN)
        std_i = math.sqrt(0.1 / INTER)
        inputs = jax.random.normal(k1, (B, S, HIDDEN), dtype=jnp.float32)
        gate_weight = jax.random.normal(k2, (NUM_EXPERTS, HIDDEN), dtype=jnp.float32) * std_h
        wi = jax.random.normal(k3, (NUM_EXPERTS, HIDDEN, INTER), dtype=jnp.float32) * std_h
        wo = jax.random.normal(k4, (NUM_EXPERTS, INTER, HIDDEN), dtype=jnp.float32) * std_i
        return {'inputs': inputs, 'gate_weight': gate_weight, 'wi': wi, 'wo': wo}
    _L0_ffn_all = _L0_ffn_setup()
    _L0_ffn_in = {k: v for k, v in _L0_ffn_all.items() if k in ('gate_weight', 'wi', 'wo')}
    del _L0_ffn_all
    return {'x': x, 'ctx_1024': ctx_1024, 'L0_xattn_Wq': _L0_xattn_in['Wq'], 'L0_xattn_bq': _L0_xattn_in['bq'], 'L0_xattn_Wk': _L0_xattn_in['Wk'], 'L0_xattn_bk': _L0_xattn_in['bk'], 'L0_ffn_gate_weight': _L0_ffn_in['gate_weight'], 'L0_ffn_wi': _L0_ffn_in['wi'], 'L0_ffn_wo': _L0_ffn_in['wo']}

def reference(x, ctx_1024, L0_xattn_Wq, L0_xattn_bq, L0_xattn_Wk, L0_xattn_bk, L0_ffn_gate_weight, L0_ffn_wi, L0_ffn_wo):
    import jax
    import jax.numpy as jnp

    def _L0_xattn_ref(teacher_logits, teacher_features, Wq, bq, Wk, bk):
        import jax, jax.numpy as jnp
        import numpy as np
        query = jnp.einsum('bnc,dc->bnd', teacher_features, Wq) + bq
        key = jnp.einsum('bnc,dc->bnd', teacher_features, Wk) + bk
        energy = jnp.einsum('bnd,bmd->bnm', query, key)
        attention = jax.nn.softmax(energy, axis=-1)
        x_m = jnp.einsum('bln,bmn->blm', teacher_logits, attention)
        return x_m

    def _L0_ffn_ref(inputs, gate_weight, wi, wo):
        import math
        import jax, jax.numpy as jnp
        import numpy as np
        NUM_EXPERTS = 8
        HIDDEN = 256
        INTER = 1024
        CAP_FACTOR = 1.25
        MIN_CAP = 4
        B, S = (4, 256)

        def _capacity(num_tokens: int, num_experts: int) -> int:
            cap = math.floor(CAP_FACTOR * num_tokens / num_experts)
            cap += cap % 2
            return max(cap, MIN_CAP)
        b, s, h = inputs.shape
        tokens = inputs.reshape(-1, h)
        T = tokens.shape[0]
        E = gate_weight.shape[0]
        C = _capacity(T, E)
        logits = tokens.astype(jnp.float32) @ gate_weight.astype(jnp.float32).T
        probs = jax.nn.softmax(logits, axis=-1)
        top1 = jnp.argmax(logits, axis=-1)
        mask = jax.nn.one_hot(top1, E, dtype=jnp.int32)
        ranks = jnp.cumsum(mask, axis=0) - 1
        mask = mask * (ranks < C).astype(jnp.int32)
        ranks_tok = jnp.sum(mask * ranks, axis=-1)
        ranks_oh = jax.nn.one_hot(ranks_tok, C, dtype=jnp.float32)
        weight = mask.astype(probs.dtype) * probs
        combine_weights = weight[:, :, None] * ranks_oh[:, None, :]
        sec_mask = jax.lax.stop_gradient(combine_weights != 0).astype(inputs.dtype)
        dispatch = jnp.einsum('tec,th->ech', sec_mask, tokens)
        hmid = jnp.einsum('ech,ehi->eci', dispatch, wi)
        hmid = jax.nn.gelu(hmid, approximate=False)
        eout = jnp.einsum('eci,eih->ech', hmid, wo)
        out = jnp.einsum('tec,ech->th', combine_weights.astype(inputs.dtype), eout)
        return out.reshape(b, s, h)
    x = x + _L0_xattn_ref(_layernorm(x, axis=-1), ctx_1024, L0_xattn_Wq, L0_xattn_bq, L0_xattn_Wk, L0_xattn_bk)
    x = x + _L0_ffn_ref(_layernorm(x, axis=-1), L0_ffn_gate_weight, L0_ffn_wi, L0_ffn_wo)
    return x

_drawn_inputs = setup_inputs


def setup_inputs(seed=0):
    import zlib

    import numpy as np

    out = dict(_drawn_inputs(seed))
    spreads = {'L0_xattn_bq': (0.0, 0.1), 'L0_xattn_bk': (0.0, 0.8)}
    factors = {'L0_ffn_gate_weight': 7.101, 'L0_ffn_wi': 6.653, 'L0_ffn_wo': 6.465}
    for name, (base, spread) in spreads.items():
        noise = np.random.default_rng([zlib.crc32(name.encode()), seed]).standard_normal(out[name].shape)
        drawn = base * np.exp(spread * noise) if base else spread * noise
        out[name] = jnp.asarray(drawn.astype(out[name].dtype))
    for name, factor in factors.items():
        out[name] = (out[name] * factor).astype(out[name].dtype)
    return out
```

```python
from contextlib import ExitStack

import concourse.bass as bass
from concourse import mybir

ALU = mybir.AluOpType
ACT = mybir.ActivationFunctionType
AX = mybir.AxisListType
F32 = mybir.dt.float32
BF16 = mybir.dt.bfloat16
I32 = mybir.dt.int32

P = 128
B = 4
S = 256
H = 256
C = 128
E = 8
F = 1024
T = B * S
NT = T // P
CAP = 160
REM = CAP - P
PER_STACK = P // REM
STACKS = E // PER_STACK
HC = H // P
IC = F // P
EPS = 1e-5
ROW = H + 4
MEAN, RSTD, INDEX, WEIGHT = H, H + 1, H + 2, H + 3
NOWHERE = 1 << 20
GROUPS = [(0, 3), (3, 6), (6, 8)]
NG = len(GROUPS)


def xattn_moe(nc, x, ctx_in, wq, bq, wk, bk, gate, wi, wo, out):
    assert CAP == (lambda c: c + c % 2)(int(1.25 * T / E))
    x_v = x.rearrange("b (t p) h -> b p t h", p=P)
    ctx_v = ctx_in.rearrange("(g b) (t p) c -> g p (b t) c", b=2, p=P)
    out_rows = out.rearrange("b s h -> (b s) h")
    out_v = out.rearrange("b (t p) h -> b p t h", p=P)
    wi_v = wi.rearrange("e (k p) i -> e p k i", p=P)
    wo_v = wo.rearrange("e (i p) h -> e p i h", p=P)

    with ExitStack() as stack:
        def sb(name, shape, dt=F32):
            return stack.enter_context(nc.sbuf_tensor(name, shape, dt))

        def sem(name):
            return stack.enter_context(nc.semaphore(name))

        bank = [stack.enter_context(nc.psum_tensor(f"bank{i}", [P, 512], F32)) for i in range(8)]

        slots_dram = nc.dram_tensor("slots_dram", [E * CAP, ROW], F32, kind="Internal").ap()

        wi_sb = sb("wi_sb", [P, E, HC, F])
        wo_sb = sb("wo_sb", [P, E, IC, H])
        shared = sb("shared", [P, 2 * HC * E * CAP + 2 * IC * CAP])

        def part(at, size, pattern, **sizes):
            assert at + size <= shared.shape[1]
            return shared[:, at:at + size].rearrange(f"p ({pattern}) -> p {pattern}", **sizes)

        x_sb = part(0, NT * H, "n h", n=NT)
        ctx_sb = part(2048, NT * C, "n c", n=NT)
        ctxT = part(3072, 4 * S, "g s", g=2)
        qT = part(4096, 4 * S, "g s", g=2)
        kT = part(5120, 4 * S, "g s", g=2)
        ln1 = part(6144, 4 * H, "b t h", b=2, t=2)
        dispT = part(0, HC * E * CAP, "k e s", k=HC, e=E)
        eoutT = part(HC * E * CAP, HC * E * P, "k e s", k=HC, e=E)
        eoutT_rem = part(HC * E * (CAP + P), HC * E * REM, "k r s", k=HC, r=STACKS)
        gelu = part(2 * HC * E * CAP, 2 * IC * CAP, "b i s", b=2, i=IC)
        rows = sb("rows", [P, NT, ROW])
        wqk = sb("wqk", [P, 2, C])
        gate_sb = sb("gate_sb", [E, H])
        bias = sb("bias", [P, 2])
        wT = sb("wT", [P, 2 * C + HC * E])
        ident = sb("ident", [P, P])
        before = sb("before", [P, P], BF16)
        ones = sb("ones", [P, P], BF16)
        lnT = sb("lnT", [P, 2, 2, S])
        att = sb("att", [P, 2, 2, S])
        attT = sb("attT", [P, 2, 2, S])
        tok = sb("tok", [P, 2, 2, H])
        stok, y = tok[:, 0, :, :], tok[:, 1, :, :]
        tokT = sb("tokT", [P, 2, 2, S])
        stats = sb("stats", [P, 2, NT, 6])
        mv = sb("mv", [P, 2, NT, 2])
        veps = sb("veps", [P, 2, NT])
        rstd1 = sb("rstd1", [P, NT])
        minus_half = sb("minus_half", [P, 2])
        nmax = sb("nmax", [P, NT])
        esum = sb("esum", [P, NT])
        erec = sb("erec", [P, NT])
        descend = sb("descend", [P, 2, E])
        lmax = sb("lmax", [P, NT])
        eq = sb("eq", [P, B, 2, E])
        z = sb("z", [P, B, 2, E])
        ez = sb("ez", [P, B, 2, E])
        zs = sb("zs", [P, NT])
        val = sb("val", [P, B, 2, E])
        vmax = sb("vmax", [P, NT])
        mask = sb("mask", [P, B, 2, E], BF16)
        seen = sb("seen", [P, B, E], BF16)
        slot0 = sb("slot0", [P, NT])
        ranked = sb("ranked", [P, B, 2, E])
        rank = sb("rank", [P, NT])
        over = sb("over", [P, NT])
        slot1 = sb("slot1", [P, NT])
        slot = sb("slot", [P, NT], I32)
        fill = sb("fill", [P, ROW])
        got = sb("got", [P, E + STACKS, ROW])

        p_wT, p_ct, p_tt = bank[0], bank[0], bank[0]
        p_q, p_gate = bank[1], bank[1]
        p_k = bank[2]
        p_en = [bank[3], bank[7]]
        p_tl, p_at, p_xm = bank[4], bank[5], bank[6]
        p_h = [bank[2], bank[3], bank[4]]
        p_e = [bank[5], bank[6]]
        p_dT = [bank[0], bank[1]]
        p_o = [bank[7]] * (E + STACKS - 1) + [bank[2]]

        x_in = [sem(f"x_in{b}") for b in range(B)]
        ctx_here = [sem(f"ctx_here{g}") for g in range(2)]
        wqk_here = sem("wqk_here")
        bias_here = sem("bias_here")
        gate_here = sem("gate_here")
        wi_here = [sem(f"wi_here{e}") for e in range(E)]
        wo_here = [sem(f"wo_here{e}") for e in range(E)]
        zeroed = sem("zeroed")
        ident_done = sem("ident_done")
        consts = sem("consts")
        fill_done = sem("fill_done")
        filled = sem("filled")
        wT_done, wT_sb = sem("wT_done"), sem("wT_sb")
        ct_done, ct_sb = sem("ct_done"), sem("ct_sb")
        q_done, q_sb = sem("q_done"), sem("q_sb")
        k_done, k_sb = sem("k_done"), sem("k_sb")
        stat1_done, pool_step, ln1_done = sem("stat1_done"), sem("pool_step"), sem("ln1_done")
        en_done, max_done, exp_done, norm_done = sem("en_done"), sem("max_done"), sem("exp_done"), sem("norm_done")
        tl_done, tl_sb = sem("tl_done"), sem("tl_sb")
        at_done, at_sb = sem("at_done"), sem("at_sb")
        xm_done, x1_done = sem("xm_done"), sem("x1_done")
        stat2_done, rstd2_done, tok_done = sem("stat2_done"), sem("rstd2_done"), sem("tok_done")
        tt_done, tt_sb = sem("tt_done"), sem("tt_sb")
        lg_done, z_done, ez_done = sem("lg_done"), sem("z_done"), sem("ez_done")
        mask_done, rk_done, slot_done = sem("mask_done"), sem("rk_done"), sem("slot_done")
        rank_read, seen_done = sem("rank_read"), sem("seen_done")
        dve_step = sem("dve_step")
        x1_out = sem("x1_out")
        scattered = sem("scattered")
        got_first, got_rem, got_rest = sem("got_first"), sem("got_rem"), sem("got_rest")
        stok_done, dT_done, dT_sb = sem("stok_done"), sem("dT_done"), sem("dT_sb")
        h_done, gelu_done = sem("h_done"), sem("gelu_done")
        e_done, e_sb = sem("e_done"), sem("e_sb")
        o_done, y_done = sem("o_done"), sem("y_done")
        y_out = [sem("y_out0"), sem("y_out1")]

        IN_TILES = [0, E] + list(range(1, PER_STACK)) + [E + 1] + list(range(PER_STACK, E))
        OUT_TILES = list(range(PER_STACK)) + [E] + list(range(PER_STACK, E)) + [E + 1]
        TILES = len(IN_TILES)
        FIRST_USE = [t if t < E else (t - E) * PER_STACK for t in IN_TILES]
        COMPLETE = [t if t < E else (t - E) * PER_STACK + PER_STACK - 1 for t in OUT_TILES]
        INS_AT = [[i for i in range(TILES) if FIRST_USE[i] == s + 1] for s in range(E + 2)]
        OUTS_AT = [[n for n in range(TILES) if COMPLETE[n] == s - 2] for s in range(E + 2)]
        FIRST_INS = [i for i in range(TILES) if FIRST_USE[i] == 0]

        block = stack.enter_context(nc.Block())

        @block.sync
        def _(sp):
            sp.dma_start(ctx_sb[:, 0:4, :], ctx_v[0]).then_inc(ctx_here[0], 16)
            sp.dma_start(x_sb[:, 0:2, :], x_v[0]).then_inc(x_in[0], 16)
            sp.dma_start(x_sb[:, 2:4, :], x_v[1]).then_inc(x_in[1], 16)
            sp.dma_start(ctx_sb[:, 4:8, :], ctx_v[1]).then_inc(ctx_here[1], 16)
            sp.dma_start(x_sb[:, 4:6, :], x_v[2]).then_inc(x_in[2], 16)
            sp.dma_start(x_sb[:, 6:8, :], x_v[3]).then_inc(x_in[3], 16)
            sp.wait_ge(fill_done, 2)
            sp.dma_start(slots_dram.rearrange("(n p) r -> p n r", p=P),
                         fill[:, None, :].to_broadcast([P, E * CAP // P, ROW])).then_inc(filled, 16)
            for e in range(E):
                sp.dma_start(wi_sb[:, e, :, :], wi_v[e]).then_inc(wi_here[e], 16)
                sp.dma_start(wo_sb[:, e, :, :], wo_v[e]).then_inc(wo_here[e], 16)

        @block.gpsimd
        def _(pool):
            steps = [0]

            def link(ins):
                steps[0] += 1
                ins.then_inc(pool_step, 1)
                pool.wait_ge(pool_step, steps[0])

            nc.gpsimd.memset(ident[:], 0.0).then_inc(zeroed, 1)
            pool.wait_ge(zeroed, 1)
            nc.gpsimd.affine_select(out=ident[:], in_=ident[:], compare_op=ALU.not_equal, fill=1.0, base=0,
                                    pattern=[[-1, P]], channel_multiplier=1).then_inc(ident_done, 1)
            nc.gpsimd.memset(fill[:], 0.0).then_inc(fill_done, 1)
            pool.wait_ge(fill_done, 1)
            nc.gpsimd.memset(fill[:, INDEX:INDEX + 1].bitcast(I32), NOWHERE).then_inc(fill_done, 1)
            nc.gpsimd.memset(minus_half[:], -0.5).then_inc(consts, 1)
            pool.wait_ge(consts, 1)

            def rstd(which, b, dst):
                v = veps[:, which, 2 * b:2 * b + 2]
                link(nc.gpsimd.tensor_scalar(v, mv[:, which, 2 * b:2 * b + 2, 1], EPS, None, ALU.add))
                return nc.gpsimd.tensor_tensor(dst, v, minus_half[:], ALU.pow)

            def first_norm(b):
                pool.wait_ge(stat1_done, b + 1)
                link(rstd(0, b, rstd1[:, 2 * b:2 * b + 2]))
                if b >= 2:
                    pool.wait_ge(tl_done, b - 1)
                for t in range(2):
                    n = 2 * b + t
                    nc.gpsimd.tensor_scalar(ln1[:, b % 2, t, :], x_sb[:, n, :], mv[:, 0, n, 0:1], rstd1[:, n:n + 1],
                                            ALU.subtract, ALU.mult).then_inc(ln1_done, 1)

            def second_rstd(b):
                pool.wait_ge(stat2_done, b + 1)
                rstd(1, b, rows[:, 2 * b:2 * b + 2, RSTD]).then_inc(rstd2_done, 1)

            def scatter(b):
                pool.wait_ge(slot_done, b + 1)
                if b == 0:
                    pool.wait_ge(filled, 16)
                for n in range(2 * b, 2 * b + 2):
                    nc.gpsimd.indirect_dma_start(
                        slots_dram, bass.IndirectOffsetOnAxis(ap=slot[:, n:n + 1], axis=0), rows[:, n, :], None,
                        bounds_check=E * CAP - 1, oob_is_err=False).then_inc(scattered, 16)

            first_norm(0)
            link(nc.gpsimd.memset(before[:], 1.0))
            nc.gpsimd.affine_select(out=before[:], in_=before[:], compare_op=ALU.is_gt, fill=0.0, base=0,
                                    pattern=[[1, P]], channel_multiplier=-1).then_inc(consts, 1)
            nc.gpsimd.memset(ones[:], 1.0).then_inc(consts, 1)
            first_norm(1)
            nc.gpsimd.iota(descend[:], pattern=[[0, 2], [-1, E]], base=E, channel_multiplier=0,
                           allow_small_or_imprecise_dtypes=True).then_inc(consts, 1)
            nc.gpsimd.iota(rows[:, :, INDEX].bitcast(I32), pattern=[[P, NT]], base=0,
                           channel_multiplier=1).then_inc(consts, 1)
            nc.gpsimd.memset(seen[:, 0, :], 0.0).then_inc(seen_done, 1)
            first_norm(2)
            second_rstd(0)
            first_norm(3)
            second_rstd(1)
            scatter(0)
            second_rstd(2)
            scatter(1)
            second_rstd(3)
            scatter(2)
            scatter(3)

            pool.wait_ge(x1_out, 16 * B)
            for n, t in enumerate(OUT_TILES):
                pool.wait_ge(y_done, n + 1)
                nc.gpsimd.indirect_dma_start(
                    out_rows, bass.IndirectOffsetOnAxis(ap=got[:, t, INDEX:INDEX + 1].bitcast(I32), axis=0),
                    y[:, n % 2, :], None, bounds_check=T - 1, oob_is_err=False).then_inc(y_out[n % 2], 16)
            for n in range(2):
                pool.wait_ge(y_out[n], 16 * (len(OUT_TILES) // 2))

        @block.scalar
        def _(act):
            act.dma_start(wqk[:, 0, :], wq).then_inc(wqk_here, 16)
            act.dma_start(wqk[:, 1, :], wk).then_inc(wqk_here, 16)
            act.dma_start(bias[:, 0:1], bq.rearrange("(d a) -> d a", a=1)).then_inc(bias_here, 16)
            act.dma_start(bias[:, 1:2], bk.rearrange("(d a) -> d a", a=1)).then_inc(bias_here, 16)
            act.dma_start(gate_sb[:], gate).then_inc(gate_here, 16)

            def copy(dst, src):
                return nc.scalar.activation(dst, src, ACT.Copy)

            def ct(g):
                act.wait_ge(ct_done, g + 1)
                copy(ctxT[:, g, :], p_ct[:]).then_inc(ct_sb, 1)

            def q(g):
                act.wait_ge(q_done, g + 1)
                if g == 0:
                    act.wait_ge(bias_here, 32)
                nc.scalar.activation(qT[:, g, :], p_q[:], ACT.Identity, bias=bias[:, 0:1]).then_inc(q_sb, 1)

            def exp(b):
                act.wait_ge(max_done, b + 1)
                if b >= 2:
                    act.wait_ge(at_done, b - 1)
                for m in range(2):
                    n = 2 * b + m
                    nc.scalar.activation(att[:, b % 2, m, :], p_en[b % 2][:, m * S:(m + 1) * S], ACT.Exp,
                                         bias=nmax[:, n:n + 1], accum_out=esum[:, n:n + 1]).then_inc(exp_done, 1)

            def tl(b):
                act.wait_ge(tl_done, b + 1)
                if b >= 2:
                    act.wait_ge(xm_done, b - 1)
                copy(lnT[:, b % 2, :, :], p_tl[:]).then_inc(tl_sb, 1)

            def at(b):
                act.wait_ge(at_done, b + 1)
                if b >= 2:
                    act.wait_ge(xm_done, b - 1)
                copy(attT[:, b % 2, :, :], p_at[:]).then_inc(at_sb, 1)

            def tt(b):
                act.wait_ge(tt_done, b + 1)
                if b >= 2:
                    act.wait_ge(lg_done, b - 1)
                copy(tokT[:, b % 2, :, :], p_tt[:]).then_inc(tt_sb, 1)

            def x1_store(b):
                act.wait_ge(x1_done, b + 1)
                act.dma_start(out_v[b], rows[:, 2 * b:2 * b + 2, 0:H]).then_inc(x1_out, 16)

            def expz(b):
                act.wait_ge(z_done, b + 1)
                nc.scalar.activation(ez[:, b, :, :], z[:, b, :, :], ACT.Exp).then_inc(ez_done, 1)

            act.wait_ge(wT_done, 1)
            copy(wT[:], p_wT[:, 0:2 * C + HC * E]).then_inc(wT_sb, 1)
            ct(0)
            q(0)
            tl(0)
            exp(0)
            exp(1)
            ct(1)
            q(1)
            tl(1)
            at(0)
            exp(2)
            x1_store(0)
            tl(2)
            at(1)
            tt(0)
            exp(3)
            expz(0)
            x1_store(1)
            tl(3)
            at(2)
            tt(1)
            expz(1)
            at(3)
            x1_store(2)
            tt(2)
            expz(2)
            x1_store(3)
            tt(3)
            expz(3)

            act.wait_ge(scattered, 16 * NT)
            by_slot = slots_dram.rearrange("(e c) r -> c e r", c=CAP)
            act.dma_start(got[:, 0:1, :], by_slot[0:P, 0:1, :]).then_inc(got_first, 16)
            for r in range(STACKS):
                for j in range(PER_STACK):
                    act.dma_start(got[j * REM:(j + 1) * REM, E + r, :],
                                  by_slot[P:CAP, r * PER_STACK + j, :]).then_inc(got_rem, 16)
            act.dma_start(got[:, 1:E, :], by_slot[0:P, 1:E, :]).then_inc(got_rest, 16)

            for e in range(E):
                for j, (a, z_) in enumerate(GROUPS):
                    act.wait_ge(h_done, NG * e + j + 1)
                    if e >= 2:
                        act.wait_ge(e_done, e - 1)
                    nc.scalar.activation(gelu[:, e % 2, a:z_, :], p_h[j][:, 0:(z_ - a) * CAP],
                                         ACT.Gelu).then_inc(gelu_done, 1)

        @block.vector
        def _(dve):
            steps = [0]

            def link(ins):
                steps[0] += 1
                ins.then_inc(dve_step, 1)
                dve.wait_ge(dve_step, steps[0])

            def moments(which, b, source):
                for t in range(2):
                    n = 2 * b + t
                    last = nc.vector.bn_stats(stats[:, which, n, :], source(n))
                link(last)
                for t in range(2):
                    n = 2 * b + t
                    last = nc.vector.bn_aggr(mv[:, which, n, :], stats[:, which, n, :])
                return last

            def st1(b):
                dve.wait_ge(x_in[b], 16)
                moments(0, b, lambda n: x_sb[:, n, :]).then_inc(stat1_done, 1)

            def k(g):
                dve.wait_ge(k_done, g + 1)
                if g == 0:
                    dve.wait_ge(bias_here, 32)
                nc.vector.tensor_scalar(kT[:, g, :], p_k[:], bias[:, 1:2], None, ALU.add).then_inc(k_sb, 1)

            def mx(b):
                dve.wait_ge(en_done, b + 1)
                nc.vector.tensor_reduce(nmax[:, 2 * b:2 * b + 2], p_en[b % 2][:].rearrange("p (m s) -> p m s", m=2),
                                        AX.X, ALU.max, negate=True).then_inc(max_done, 1)

            def norm(b):
                dve.wait_ge(exp_done, 2 * b + 2)
                link(nc.vector.reciprocal(erec[:, 2 * b:2 * b + 2], esum[:, 2 * b:2 * b + 2]))
                for m in range(2):
                    n = 2 * b + m
                    nc.vector.tensor_scalar(att[:, b % 2, m, :], att[:, b % 2, m, :], erec[:, n:n + 1], None,
                                            ALU.mult).then_inc(norm_done, 1)

            def x1(b):
                dve.wait_ge(xm_done, b + 1)
                pair = slice(2 * b, 2 * b + 2)
                nc.vector.tensor_tensor(rows[:, pair, 0:H], p_xm[:].rearrange("p (t h) -> p t h", t=2),
                                        x_sb[:, pair, :], ALU.add).then_inc(x1_done, 1)
                dve.wait_ge(x1_done, b + 1)
                link(moments(1, b, lambda n: rows[:, n, 0:H]))
                nc.vector.tensor_copy(rows[:, pair, MEAN], mv[:, 1, pair, 0]).then_inc(stat2_done, 1)

            def tk(b):
                dve.wait_ge(rstd2_done, b + 1)
                if b >= 2:
                    dve.wait_ge(tt_done, b - 1)
                for t in range(2):
                    n = 2 * b + t
                    nc.vector.tensor_scalar(tok[:, b % 2, t, :], rows[:, n, 0:H], mv[:, 1, n, 0:1],
                                            rows[:, n, RSTD:RSTD + 1], ALU.subtract, ALU.mult).then_inc(tok_done, 1)

            def wide(v):
                return v[:, :, None].to_broadcast([P, 2, E])

            def route(b):
                pair = slice(2 * b, 2 * b + 2)
                logits = p_gate[:, 0:2 * E].rearrange("p (t e) -> p t e", t=2)
                if b == 0:
                    dve.wait_ge(consts, 5)
                dve.wait_ge(lg_done, b + 1)
                link(nc.vector.tensor_reduce(lmax[:, pair], logits, AX.X, ALU.max))
                nc.vector.tensor_tensor(z[:, b, :, :], logits, wide(lmax[:, pair]), ALU.subtract).then_inc(z_done, 1)
                link(nc.vector.tensor_tensor(eq[:, b, :, :], logits, wide(lmax[:, pair]), ALU.is_equal))
                link(nc.vector.tensor_tensor(val[:, b, :, :], eq[:, b, :, :], descend[:], ALU.mult))
                link(nc.vector.tensor_reduce(vmax[:, pair], val[:, b, :, :], AX.X, ALU.max))
                nc.vector.tensor_tensor(mask[:, b, :, :], val[:, b, :, :], wide(vmax[:, pair]),
                                        ALU.is_equal).then_inc(mask_done, 1)
                nc.vector.tensor_scalar(slot0[:, pair], vmax[:, pair], -float(CAP), float(E * CAP), ALU.mult, ALU.add)
                if b + 1 < B:
                    dve.wait_ge(mask_done, b + 1)
                    dve.wait_ge(seen_done, b + 1)
                    link(nc.vector.tensor_tensor(seen[:, b + 1, :], seen[:, b, :], mask[:, b, 0, :], ALU.add))
                    nc.vector.tensor_tensor(seen[:, b + 1, :], seen[:, b + 1, :], mask[:, b, 1, :],
                                            ALU.add).then_inc(seen_done, 1)

            def place(b):
                pair = slice(2 * b, 2 * b + 2)
                dve.wait_ge(ez_done, b + 1)
                link(nc.vector.tensor_reduce(zs[:, pair], ez[:, b, :, :], AX.X, ALU.add))
                nc.vector.reciprocal(rows[:, pair, WEIGHT], zs[:, pair])
                dve.wait_ge(rk_done, b + 1)
                ranks = p_gate[:, 64:64 + 2 * E].rearrange("p (t e) -> p t e", t=2)
                nc.vector.tensor_tensor(ranked[:, b, :, :], ranks, mask[:, b, :, :], ALU.mult).then_inc(rank_read, 1)
                dve.wait_ge(rank_read, b + 1)
                link(nc.vector.tensor_reduce(rank[:, pair], ranked[:, b, :, :], AX.X, ALU.add))
                nc.vector.tensor_scalar(over[:, pair], rank[:, pair], float(CAP), float(NOWHERE), ALU.is_ge, ALU.mult)
                link(nc.vector.tensor_tensor(slot1[:, pair], rank[:, pair], slot0[:, pair], ALU.add))
                nc.vector.tensor_tensor(slot[:, pair], slot1[:, pair], over[:, pair], ALU.add).then_inc(slot_done, 1)

            st1(0)
            st1(1)
            k(0)
            mx(0)
            mx(1)
            st1(2)
            norm(0)
            k(1)
            norm(1)
            st1(3)
            x1(0)
            mx(2)
            tk(0)
            norm(2)
            x1(1)
            route(0)
            mx(3)
            tk(1)
            place(0)
            norm(3)
            x1(2)
            route(1)
            tk(2)
            place(1)
            x1(3)
            route(2)
            tk(3)
            place(2)
            route(3)
            place(3)

            def load_tile(i):
                t = IN_TILES[i]
                if i == 0:
                    dve.wait_ge(got_first, 16)
                elif i == 1:
                    dve.wait_ge(got_rem, 16 * E)
                elif i == 2:
                    dve.wait_ge(got_rest, 16)
                if i >= 2:
                    dve.wait_ge(dT_done, i - 1)
                nc.vector.tensor_scalar(stok[:, i % 2, :], got[:, t, 0:H], got[:, t, MEAN:MEAN + 1],
                                        got[:, t, RSTD:RSTD + 1], ALU.subtract, ALU.mult).then_inc(stok_done, 1)

            def load_tileT(i):
                t = IN_TILES[i]
                dve.wait_ge(dT_done, i + 1)
                if t < E:
                    nc.vector.tensor_copy(dispT[:, :, t, 0:P], p_dT[i % 2][:, 0:H].rearrange(
                        "p (c s) -> p c s", c=HC)).then_inc(dT_sb, 1)
                else:
                    first = (t - E) * PER_STACK
                    nc.vector.tensor_copy(dispT[:, :, first:first + PER_STACK, P:CAP], p_dT[i % 2][:, 0:H].rearrange(
                        "p (c j s) -> p c j s", c=HC, j=PER_STACK)).then_inc(dT_sb, 1)
                if i + 2 < TILES:
                    load_tile(i + 2)

            def out_tile(n):
                t = OUT_TILES[n]
                dve.wait_ge(o_done, n + 1)
                if n >= 2:
                    dve.wait_ge(y_out[n % 2], 16 * (n // 2))
                nc.vector.scalar_tensor_tensor(y[:, n % 2, :], p_o[n][:, 0:H], got[:, t, WEIGHT:WEIGHT + 1],
                                               got[:, t, 0:H], ALU.mult, ALU.add).then_inc(y_done, 1)

            def expert_out(e):
                dve.wait_ge(e_done, e + 1)
                src = p_e[e % 2][:, 0:HC * CAP].rearrange("p (c s) -> p c s", c=HC)
                r, j = e // PER_STACK, e % PER_STACK
                nc.vector.tensor_copy(eoutT[:, :, e, :], src[:, :, 0:P])
                nc.vector.tensor_copy(eoutT_rem[:, :, r, j * REM:(j + 1) * REM], src[:, :, P:CAP]).then_inc(e_sb, 1)

            load_tile(0)
            load_tile(1)
            for i in FIRST_INS:
                load_tileT(i)
            for s in range(E + 2):
                for i in INS_AT[s]:
                    load_tileT(i)
                for n in OUTS_AT[s]:
                    out_tile(n)
                if 1 <= s <= E:
                    expert_out(s - 1)

        @block.tensor
        def _(pe):
            def turn(dst, src, n=P):
                return nc.tensor.transpose(dst, src, ident[0:n, 0:n])

            def mm(dst, lhsT, rhs, k, last):
                return nc.tensor.matmul(dst, lhsT, rhs, start=(k == 0), stop=last)

            def ct(g):
                pe.wait_ge(ctx_here[g], 16)
                if g == 0:
                    pe.wait_ge(wT_sb, 1)
                else:
                    pe.wait_ge(ct_sb, g)
                for n in range(4):
                    last = turn(p_ct[:, n * P:(n + 1) * P], ctx_sb[:, 4 * g + n, :])
                last.then_inc(ct_done, 1)

            def qk(g):
                pe.wait_ge(ct_sb, g + 1)
                if g:
                    pe.wait_ge(q_sb, g)
                mm(p_q[:], wT[:, 0:C], ctxT[:, g, :], 0, True).then_inc(q_done, 1)
                if g:
                    pe.wait_ge(k_sb, g)
                mm(p_k[:], wT[:, C:2 * C], ctxT[:, g, :], 0, True).then_inc(k_done, 1)

            def en(b):
                g, o = b // 2, (b % 2) * S
                pe.wait_ge(q_sb, g + 1)
                pe.wait_ge(k_sb, g + 1)
                if b >= 2:
                    pe.wait_ge(exp_done, 2 * (b - 1))
                for m in range(2):
                    last = mm(p_en[b % 2][:, m * S:(m + 1) * S], qT[:, g, o + m * P:o + (m + 1) * P],
                              kT[:, g, o:o + S], 0, True)
                last.then_inc(en_done, 1)

            def tl(b):
                pe.wait_ge(ln1_done, 2 * b + 2)
                if b:
                    pe.wait_ge(tl_sb, b)
                for c in range(2):
                    for t in range(2):
                        last = turn(p_tl[:, c * S + t * P:c * S + (t + 1) * P], ln1[:, b % 2, t, c * P:(c + 1) * P])
                last.then_inc(tl_done, 1)

            def at(b):
                pe.wait_ge(norm_done, 2 * b + 2)
                if b:
                    pe.wait_ge(at_sb, b)
                for c in range(2):
                    for m in range(2):
                        last = turn(p_at[:, c * S + m * P:c * S + (m + 1) * P], att[:, b % 2, m, c * P:(c + 1) * P])
                last.then_inc(at_done, 1)

            def xm(b):
                pe.wait_ge(at_sb, b + 1)
                pe.wait_ge(tl_sb, b + 1)
                if b:
                    pe.wait_ge(x1_done, b)
                for t in range(2):
                    for c in range(2):
                        last = mm(p_xm[:, t * H:(t + 1) * H], lnT[:, b % 2, c, t * P:(t + 1) * P],
                                  attT[:, b % 2, c, :], c, c == 1)
                last.then_inc(xm_done, 1)

            def tt(b):
                pe.wait_ge(tok_done, 2 * b + 2)
                if b:
                    pe.wait_ge(tt_sb, b)
                for c in range(HC):
                    for t in range(2):
                        last = turn(p_tt[:, c * S + t * P:c * S + (t + 1) * P], tok[:, b % 2, t, c * P:(c + 1) * P])
                last.then_inc(tt_done, 1)

            def lg(b):
                pe.wait_ge(tt_sb, b + 1)
                if b == 0:
                    pe.wait_ge(q_sb, 2)
                else:
                    pe.wait_ge(rank_read, b)
                for t in range(2):
                    for c in range(HC):
                        last = mm(p_gate[:, t * E:(t + 1) * E], tokT[:, b % 2, c, t * P:(t + 1) * P],
                                  wT[:, 2 * C + c * E:2 * C + (c + 1) * E], c, c == HC - 1)
                last.then_inc(lg_done, 1)

            def rk(b):
                pe.wait_ge(mask_done, b + 1)
                r = p_gate[:, 64:64 + 2 * E]
                pe.wait_ge(seen_done, b + 1)
                nc.tensor.matmul(r, before[:], mask[:, b, :, :], start=True, stop=False, skip_group_check=True)
                for t in range(2):
                    nc.tensor.matmul(r[:, t * E:(t + 1) * E], ones[:], seen[:, b, :], start=False, stop=False,
                                     skip_group_check=True)
                nc.tensor.matmul(r[:, E:2 * E], ones[:], mask[:, b, 0, :], start=False, stop=True,
                                 skip_group_check=True).then_inc(rk_done, 1)

            pe.wait_ge(ident_done, 1)
            pe.wait_ge(wqk_here, 32)
            pe.wait_ge(gate_here, 16)
            for w in range(2):
                turn(p_wT[:, w * C:(w + 1) * C], wqk[:, w, :])
            for c in range(HC):
                last = turn(p_wT[:, 2 * C + c * E:2 * C + (c + 1) * E], gate_sb[:, c * P:(c + 1) * P], E)
            last.then_inc(wT_done, 1)
            ct(0)
            qk(0)
            en(0)
            tl(0)
            en(1)
            ct(1)
            qk(1)
            tl(1)
            at(0)
            xm(0)
            en(2)
            tl(2)
            at(1)
            xm(1)
            tt(0)
            lg(0)
            en(3)
            tl(3)
            rk(0)
            at(2)
            xm(2)
            tt(1)
            lg(1)
            at(3)
            rk(1)
            xm(3)
            tt(2)
            lg(2)
            rk(2)
            tt(3)
            lg(3)
            rk(3)

            def dT(i):
                pe.wait_ge(stok_done, i + 1)
                if i >= 2:
                    pe.wait_ge(dT_sb, i - 1)
                for c in range(HC):
                    last = turn(p_dT[i % 2][:, c * P:(c + 1) * P], stok[:, i % 2, c * P:(c + 1) * P])
                last.then_inc(dT_done, 1)

            def mm1(e):
                pe.wait_ge(wi_here[e], 16)
                pe.wait_ge(dT_sb, max(i for i in range(TILES) if FIRST_USE[i] <= e) + 1)
                for j, (a, z_) in enumerate(GROUPS):
                    if e:
                        pe.wait_ge(gelu_done, NG * (e - 1) + j + 1)
                    for i in range(a, z_):
                        for c in range(HC):
                            last = mm(p_h[j][:, (i - a) * CAP:(i - a + 1) * CAP], wi_sb[:, e, c, i * P:(i + 1) * P],
                                      dispT[:, c, e, :], c, c == HC - 1)
                    last.then_inc(h_done, 1)

            def mm2(e):
                pe.wait_ge(wo_here[e], 16)
                pe.wait_ge(gelu_done, NG * (e + 1))
                if e >= 2:
                    pe.wait_ge(e_sb, e - 1)
                for c in range(HC):
                    for i in range(IC):
                        last = mm(p_e[e % 2][:, c * CAP:(c + 1) * CAP], wo_sb[:, e, i, c * P:(c + 1) * P],
                                  gelu[:, e % 2, i, :], i, i == IC - 1)
                last.then_inc(e_done, 1)

            def oT(n):
                t = OUT_TILES[n]
                pe.wait_ge(e_sb, COMPLETE[n] + 1)
                if n == TILES - 1:
                    pe.wait_ge(gelu_done, NG * E)
                elif n:
                    pe.wait_ge(y_done, n)
                for c in range(HC):
                    src = eoutT[:, c, t, :] if t < E else eoutT_rem[:, c, t - E, :]
                    last = turn(p_o[n][:, c * P:(c + 1) * P], src)
                last.then_inc(o_done, 1)

            for i in FIRST_INS:
                dT(i)
            for s in range(E + 2):
                for i in INS_AT[s]:
                    dT(i)
                if s < E:
                    mm1(s)
                for n in OUTS_AT[s]:
                    oT(n)
                if 1 <= s <= E:
                    mm2(s - 1)


_INS = ["x", "ctx_1024", "L0_xattn_Wq", "L0_xattn_bq", "L0_xattn_Wk", "L0_xattn_bk", "L0_ffn_gate_weight",
        "L0_ffn_wi", "L0_ffn_wo"]


def kernel(**inputs):
    import numpy as _np
    import concourse.bacc as _bacc
    from concourse import mybir as _mybir
    from concourse.bass_utils import run_bass_kernel_spmd as _run

    nc = _bacc.Bacc("TRN2", target_bir_lowering=False, num_devices=1)
    arrays, args = {}, []
    for name in _INS:
        a = _np.ascontiguousarray(inputs[name])
        arrays[f"in_{name}"] = a
        args.append(nc.dram_tensor(f"in_{name}", a.shape, _mybir.dt.from_np(a.dtype), kind="ExternalInput").ap())
    args.append(nc.dram_tensor("out_0", (B, S, H), F32, kind="ExternalOutput").ap())
    xattn_moe(nc, *args)
    r = _run(nc, [arrays], core_ids=[0])
    return r.results[0]["out_0"]
```

```python
from contextlib import ExitStack

import concourse.bass as bass
from concourse import mybir

ALU = mybir.AluOpType
ACT = mybir.ActivationFunctionType
AX = mybir.AxisListType
F32 = mybir.dt.float32
BF16 = mybir.dt.bfloat16
I32 = mybir.dt.int32

P = 128
B = 4
S = 256
H = 256
C = 128
E = 8
F = 1024
T = B * S
NT = T // P
CAP = 160
REM = CAP - P
PER_STACK = P // REM
STACKS = E // PER_STACK
HC = H // P
IC = F // P
EPS = 1e-5
ROW = H + 4
MEAN, RSTD, INDEX, WEIGHT = H, H + 1, H + 2, H + 3
NOWHERE = 1 << 20
GROUPS = [(0, 3), (3, 6), (6, 8)]
NG = len(GROUPS)
WARM_START = 6
WARM_DISPATCH = 22


def xattn_moe(nc, x, ctx_in, wq, bq, wk, bk, gate, wi, wo, out):
    assert CAP == (lambda c: c + c % 2)(int(1.25 * T / E))
    x_v = x.rearrange("b (t p) h -> b p t h", p=P)
    ctx_v = ctx_in.rearrange("(g b) (t p) c -> g p (b t) c", b=2, p=P)
    out_rows = out.rearrange("b s h -> (b s) h")
    out_v = out.rearrange("b (t p) h -> b p t h", p=P)
    wi_v = wi.rearrange("e (k p) i -> e p k i", p=P)
    wo_v = wo.rearrange("e (i p) h -> e p i h", p=P)

    with ExitStack() as stack:
        def sb(name, shape, dt=F32):
            return stack.enter_context(nc.sbuf_tensor(name, shape, dt))

        def sem(name):
            return stack.enter_context(nc.semaphore(name))

        bank = [stack.enter_context(nc.psum_tensor(f"bank{i}", [P, 512], F32)) for i in range(8)]

        slots_dram = nc.dram_tensor("slots_dram", [E * CAP, ROW], F32, kind="Internal").ap()
        by_rank = slots_dram.rearrange("(c e) r -> c e r", e=E)

        wi_sb = sb("wi_sb", [P, E, HC, F])
        wo_sb = sb("wo_sb", [P, E, IC, H])
        RING = PER_STACK + 1
        shared = sb("shared", [P, HC * E * CAP + RING * IC * CAP + P * 2])

        def part(at, size, pattern, **sizes):
            assert at + size <= shared.shape[1]
            return shared[:, at:at + size].rearrange(f"p ({pattern}) -> p {pattern}", **sizes)

        x_sb = part(0, NT * H, "n h", n=NT)
        ctx_sb = part(2048, NT * C, "n c", n=NT)
        ctxT = part(3072, 4 * S, "g s", g=2)
        qT = part(4096, 4 * S, "g s", g=2)
        kT = part(5120, 4 * S, "g s", g=2)
        ln1 = part(6144, 4 * H, "b t h", b=2, t=2)
        att = part(7168, 4 * S, "b t s", b=2, t=2)
        lnT = part(8192, 4 * S, "b t s", b=2, t=2)
        dispT = part(0, HC * E * CAP, "k e s", k=HC, e=E)
        gelu = part(HC * E * CAP, RING * IC * CAP, "b i s", b=RING, i=IC)
        rows = sb("rows", [P, NT, ROW])
        wqk = sb("wqk", [P, 2, C])
        gate_sb = sb("gate_sb", [E, H])
        bias = sb("bias", [P, 2])
        wT = sb("wT", [P, 2 * C])
        gateT = sb("gateT", [P, HC, E])
        ident = sb("ident", [P, P])
        before = sb("before", [P, P], BF16)
        ones = sb("ones", [P, P], BF16)
        attT = sb("attT", [P, 2, 2, S])
        tok = sb("tok", [P, 2, 2, H])
        stok, y = tok[:, 0, :, :], tok[:, 1, :, :]
        tokT = sb("tokT", [P, 2, 2, S])
        stats = sb("stats", [P, 2, NT, 6])
        mv = sb("mv", [P, 2, NT, 2])
        veps = sb("veps", [P, 2, NT])
        rstd1 = sb("rstd1", [P, NT])
        minus_half = sb("minus_half", [P, 2])
        nmax = sb("nmax", [P, NT])
        esum = sb("esum", [P, NT])
        erec = sb("erec", [P, NT])
        descend = sb("descend", [P, 2, E])
        logits = sb("logits", [P, B, 2, E])
        lmax = sb("lmax", [P, NT])
        nlmax = sb("nlmax", [P, NT])
        ez = sb("ez", [P, NT, E])
        zs = sb("zs", [P, NT])
        val = sb("val", [P, B, 2, E])
        vmax = sb("vmax", [P, NT])
        expert = sb("expert", [P, NT])
        mask = sb("mask", [P, B, 2, E], BF16)
        seen = sb("seen", [P, B, E], BF16)
        ranked = sb("ranked", [P, NT, E])
        rank = sb("rank", [P, NT])
        slot = sb("slot", [P, NT], I32)
        fill = sb("fill", [P, ROW])
        got = sb("got", [P, E + STACKS, ROW])

        p_wT, p_ct, p_gt = bank[0], bank[0], bank[0]
        p_tt = [bank[0], bank[2]]
        p_q, p_gate = bank[1], bank[1]
        p_k = bank[2]
        p_en = [bank[3], bank[7]]
        p_tl, p_at, p_xm = bank[4], bank[5], bank[6]
        p_h = [bank[2], bank[3], bank[4]]
        p_dT = [bank[0], bank[1]]
        p_o = [bank[5], bank[6]]
        p_warm = bank[7]

        x_in = [sem(f"x_in{b}") for b in range(B)]
        ctx_here = [sem(f"ctx_here{g}") for g in range(2)]
        wqk_here = sem("wqk_here")
        bias_here = sem("bias_here")
        gate_here = sem("gate_here")
        wi_here = [sem(f"wi_here{e}") for e in range(E)]
        wo_here = [sem(f"wo_here{e}") for e in range(E)]
        zeroed = sem("zeroed")
        ident_done = sem("ident_done")
        consts = sem("consts")
        fill_done = sem("fill_done")
        filled = sem("filled")
        wT_done, wT_sb = sem("wT_done"), sem("wT_sb")
        gt_done, gt_sb = sem("gt_done"), sem("gt_sb")
        ct_done, ct_sb = sem("ct_done"), sem("ct_sb")
        q_done, q_sb = sem("q_done"), sem("q_sb")
        k_done, k_sb = sem("k_done"), sem("k_sb")
        stat1_done, rstd1_done, ln1_done = sem("stat1_done"), sem("rstd1_done"), sem("ln1_done")
        en_done, max_done, exp_done, norm_done = sem("en_done"), sem("max_done"), sem("exp_done"), sem("norm_done")
        tl_done, tl_sb = sem("tl_done"), sem("tl_sb")
        at_done, at_sb = sem("at_done"), sem("at_sb")
        xm_done, x1_done = sem("xm_done"), sem("x1_done")
        stat2_done, rstd2_done, tok_done = sem("stat2_done"), sem("rstd2_done"), sem("tok_done")
        tt_done, tt_sb = sem("tt_done"), sem("tt_sb")
        lg_done, lmax_done, zs_done = sem("lg_done"), sem("lmax_done"), sem("zs_done")
        mask_done, rk_done, slot_done = sem("mask_done"), sem("rk_done"), sem("slot_done")
        rank_read, seen_done = sem("rank_read"), sem("seen_done")
        dve_step = sem("dve_step")
        x1_out = sem("x1_out")
        scattered = sem("scattered")
        got_first, got_main, got_rem = sem("got_first"), sem("got_main"), sem("got_rem")
        stok_done, dT_done, dT_sb = sem("stok_done"), sem("dT_done"), sem("dT_sb")
        h_done, gelu_done = sem("h_done"), sem("gelu_done")
        o_done, y_done = sem("o_done"), sem("y_done")
        y_out = [sem("y_out0"), sem("y_out1")]

        IN_TILES = [0, E] + list(range(1, PER_STACK)) + [E + 1] + list(range(PER_STACK, E))
        OUT_TILES = list(range(PER_STACK)) + [E] + list(range(PER_STACK, E)) + [E + 1]
        TILES = len(IN_TILES)
        FIRST_USE = [t if t < E else (t - E) * PER_STACK for t in IN_TILES]
        INS_AT = [[i for i in range(TILES) if FIRST_USE[i] == s + 1] for s in range(E + 1)]
        FIRST_INS = [i for i in range(TILES) if FIRST_USE[i] == 0]

        def last_slots(queue, r):
            first = r * PER_STACK
            queue.dma_start(got[:, E + r, :],
                            by_rank[P:CAP, first:first + PER_STACK, :].rearrange("q j w -> j q w")).then_inc(got_rem, 16)

        block = stack.enter_context(nc.Block())

        @block.sync
        def _(sp):
            def weights(e):
                sp.dma_start(wi_sb[:, e, :, :], wi_v[e]).then_inc(wi_here[e], 16)
                sp.dma_start(wo_sb[:, e, :, :], wo_v[e]).then_inc(wo_here[e], 16)

            sp.dma_start(wqk[:, 0, :], wq).then_inc(wqk_here, 16)
            sp.dma_start(wqk[:, 1, :], wk).then_inc(wqk_here, 16)
            sp.dma_start(ctx_sb[:, 0:4, :], ctx_v[0]).then_inc(ctx_here[0], 16)
            sp.dma_start(x_sb[:, 0:2, :], x_v[0]).then_inc(x_in[0], 16)
            sp.dma_start(x_sb[:, 2:4, :], x_v[1]).then_inc(x_in[1], 16)
            sp.dma_start(gate_sb[:], gate).then_inc(gate_here, 16)
            sp.dma_start(ctx_sb[:, 4:8, :], ctx_v[1]).then_inc(ctx_here[1], 16)
            sp.dma_start(x_sb[:, 4:6, :], x_v[2]).then_inc(x_in[2], 16)
            sp.dma_start(x_sb[:, 6:8, :], x_v[3]).then_inc(x_in[3], 16)
            sp.wait_ge(fill_done, 2)
            sp.dma_start(slots_dram.rearrange("(n p) r -> p n r", p=P),
                         fill[:, None, :].to_broadcast([P, E * CAP // P, ROW])).then_inc(filled, 16)
            weights(0)
            weights(1)
            sp.wait_ge(x1_done, 1)
            weights(2)
            sp.wait_ge(x1_done, 3)
            weights(3)

            sp.wait_ge(scattered, 16 * NT)
            sp.dma_start(got[:, 0, :], by_rank[0:P, 0, :]).then_inc(got_first, 16)
            last_slots(sp, 1)
            sp.wait_ge(got_main, 16)
            weights(4)
            for b in range(B):
                sp.dma_start(out_v[b], rows[:, 2 * b:2 * b + 2, 0:H]).then_inc(x1_out, 16)
            for e in range(5, E):
                weights(e)

        @block.gpsimd
        def _(pool):
            nc.gpsimd.memset(ident[:], 0.0).then_inc(zeroed, 1)
            pool.wait_ge(zeroed, 1)
            nc.gpsimd.affine_select(out=ident[:], in_=ident[:], compare_op=ALU.not_equal, fill=1.0, base=0,
                                    pattern=[[-1, P]], channel_multiplier=1).then_inc(ident_done, 1)
            nc.gpsimd.memset(fill[:], 0.0).then_inc(fill_done, 1)
            pool.wait_ge(fill_done, 1)
            nc.gpsimd.memset(fill[:, INDEX:INDEX + 1].bitcast(I32), NOWHERE).then_inc(fill_done, 1)
            nc.gpsimd.memset(minus_half[:], -0.5).then_inc(consts, 1)
            pool.wait_ge(consts, 1)

            def first_rstd(b):
                pool.wait_ge(stat1_done, b + 1)
                nc.gpsimd.tensor_tensor(rstd1[:, 2 * b:2 * b + 2], veps[:, 0, 2 * b:2 * b + 2], minus_half[:],
                                        ALU.pow).then_inc(rstd1_done, 1)

            def second_rstd(b):
                pool.wait_ge(stat2_done, b + 1)
                nc.gpsimd.tensor_tensor(rows[:, 2 * b:2 * b + 2, RSTD], veps[:, 1, 2 * b:2 * b + 2], minus_half[:],
                                        ALU.pow).then_inc(rstd2_done, 1)

            def scatter(b):
                pool.wait_ge(slot_done, b + 1)
                if b == 0:
                    pool.wait_ge(filled, 16)
                for n in range(2 * b, 2 * b + 2):
                    nc.gpsimd.indirect_dma_start(
                        slots_dram, bass.IndirectOffsetOnAxis(ap=slot[:, n:n + 1], axis=0), rows[:, n, :], None,
                        bounds_check=E * CAP - 1, oob_is_err=False).then_inc(scattered, 16)

            nc.gpsimd.memset(before[:], 1.0).then_inc(zeroed, 1)
            nc.gpsimd.memset(ones[:], 1.0).then_inc(consts, 1)
            pool.wait_ge(zeroed, 2)
            nc.gpsimd.affine_select(out=before[:], in_=before[:], compare_op=ALU.is_gt, fill=0.0, base=0,
                                    pattern=[[1, P]], channel_multiplier=-1).then_inc(consts, 1)
            nc.gpsimd.iota(descend[:], pattern=[[0, 2], [-1, E]], base=E, channel_multiplier=0,
                           allow_small_or_imprecise_dtypes=True).then_inc(consts, 1)
            nc.gpsimd.iota(rows[:, :, INDEX].bitcast(I32), pattern=[[P, NT]], base=0,
                           channel_multiplier=1).then_inc(consts, 1)
            nc.gpsimd.memset(seen[:, 0, :], 0.0).then_inc(seen_done, 1)
            first_rstd(0)
            first_rstd(1)
            first_rstd(2)
            first_rstd(3)
            second_rstd(0)
            second_rstd(1)
            scatter(0)
            second_rstd(2)
            scatter(1)
            second_rstd(3)
            scatter(2)
            scatter(3)

            pool.wait_ge(x1_out, 16 * B)
            for n, t in enumerate(OUT_TILES):
                pool.wait_ge(y_done, n + 1)
                nc.gpsimd.indirect_dma_start(
                    out_rows, bass.IndirectOffsetOnAxis(ap=got[:, t, INDEX:INDEX + 1].bitcast(I32), axis=0),
                    y[:, n % 2, :], None, bounds_check=T - 1, oob_is_err=False).then_inc(y_out[n % 2], 16)
            for n in range(2):
                pool.wait_ge(y_out[n], 16 * (len(OUT_TILES) // 2))

        @block.scalar
        def _(act):
            act.dma_start(bias[:, 0:1], bq.rearrange("(d a) -> d a", a=1)).then_inc(bias_here, 16)
            act.dma_start(bias[:, 1:2], bk.rearrange("(d a) -> d a", a=1)).then_inc(bias_here, 16)
            nc.scalar.preload_act_table(ACT.Exp)

            def copy(dst, src):
                return nc.scalar.activation(dst, src, ACT.Copy)

            def ct(g):
                act.wait_ge(ct_done, g + 1)
                copy(ctxT[:, g, :], p_ct[:]).then_inc(ct_sb, 1)

            def q(g):
                act.wait_ge(q_done, g + 1)
                if g == 0:
                    act.wait_ge(bias_here, 32)
                nc.scalar.activation(qT[:, g, :], p_q[:], ACT.Identity, bias=bias[:, 0:1]).then_inc(q_sb, 1)

            def k(g):
                act.wait_ge(k_done, g + 1)
                nc.scalar.activation(kT[:, g, :], p_k[:], ACT.Identity, bias=bias[:, 1:2]).then_inc(k_sb, 1)

            def exp(b):
                act.wait_ge(max_done, b + 1)
                if b >= 2:
                    act.wait_ge(at_done, b - 1)
                for m in range(2):
                    n = 2 * b + m
                    nc.scalar.activation(att[:, b % 2, m, :], p_en[b % 2][:, m * S:(m + 1) * S], ACT.Exp,
                                         bias=nmax[:, n:n + 1], accum_out=esum[:, n:n + 1]).then_inc(exp_done, 1)

            def tl(b):
                act.wait_ge(tl_done, b + 1)
                if b >= 2:
                    act.wait_ge(xm_done, b - 1)
                copy(lnT[:, b % 2, :, :], p_tl[:]).then_inc(tl_sb, 1)

            def at(b):
                act.wait_ge(at_done, b + 1)
                if b >= 2:
                    act.wait_ge(xm_done, b - 1)
                copy(attT[:, b % 2, :, :], p_at[:]).then_inc(at_sb, 1)

            def tt(b):
                act.wait_ge(tt_done, b + 1)
                if b >= 2:
                    act.wait_ge(lg_done, b - 1)
                copy(tokT[:, b % 2, :, :], p_tt[b % 2][:]).then_inc(tt_sb, 1)

            def expz(b):
                act.wait_ge(lmax_done, 2 * b + 2)
                for n in range(2 * b, 2 * b + 2):
                    nc.scalar.activation(ez[:, n, :], logits[:, b, n % 2, :], ACT.Exp, bias=nlmax[:, n:n + 1],
                                         accum_out=zs[:, n:n + 1]).then_inc(zs_done, 1)

            def gt():
                act.wait_ge(gt_done, 1)
                copy(gateT[:], p_gt[:, 0:HC * E]).then_inc(gt_sb, 1)

            act.wait_ge(wT_done, 1)
            copy(wT[:], p_wT[:, 0:2 * C]).then_inc(wT_sb, 1)
            ct(0)
            q(0)
            k(0)
            ct(1)
            exp(0)
            tl(0)
            q(1)
            exp(1)
            at(0)
            tl(1)
            k(1)
            at(1)
            gt()
            exp(2)
            tl(2)
            tt(0)
            at(2)
            expz(0)
            exp(3)
            tl(3)
            tt(1)
            at(3)
            expz(1)
            tt(2)
            expz(2)
            tt(3)
            expz(3)
            nc.scalar.preload_act_table(ACT.Gelu)

            act.wait_ge(scattered, 16 * NT)
            last_slots(act, 0)
            act.dma_start(got[:, 1:E, :], by_rank[0:P, 1:E, :]).then_inc(got_main, 16)

            for e in range(E):
                if e >= RING:
                    act.wait_ge(o_done, PER_STACK + 1)
                for j, (a, z) in enumerate(GROUPS):
                    act.wait_ge(h_done, NG * e + j + 1)
                    nc.scalar.activation(gelu[:, e % RING, a:z, :], p_h[j][:, 0:(z - a) * CAP],
                                         ACT.Gelu).then_inc(gelu_done, 1)

        @block.vector
        def _(dve):
            steps = [0]

            def link(ins):
                steps[0] += 1
                ins.then_inc(dve_step, 1)
                dve.wait_ge(dve_step, steps[0])

            def moments(which, b, source):
                for t in range(2):
                    n = 2 * b + t
                    last = nc.vector.bn_stats(stats[:, which, n, :], source(n))
                link(last)
                for t in range(2):
                    n = 2 * b + t
                    last = nc.vector.bn_aggr(mv[:, which, n, :], stats[:, which, n, :])
                link(last)
                pair = slice(2 * b, 2 * b + 2)
                return nc.vector.tensor_scalar(veps[:, which, pair], mv[:, which, pair, 1], EPS, None, ALU.add)

            def st1(b):
                dve.wait_ge(x_in[b], 16)
                moments(0, b, lambda n: x_sb[:, n, :]).then_inc(stat1_done, 1)

            def ln(b):
                dve.wait_ge(rstd1_done, b + 1)
                if b >= 2:
                    dve.wait_ge(tl_done, b - 1)
                for t in range(2):
                    n = 2 * b + t
                    nc.vector.tensor_scalar(ln1[:, b % 2, t, :], x_sb[:, n, :], mv[:, 0, n, 0:1], rstd1[:, n:n + 1],
                                            ALU.subtract, ALU.mult).then_inc(ln1_done, 1)

            def mx(b):
                dve.wait_ge(en_done, b + 1)
                nc.vector.tensor_reduce(nmax[:, 2 * b:2 * b + 2], p_en[b % 2][:].rearrange("p (m s) -> p m s", m=2),
                                        AX.X, ALU.max, negate=True).then_inc(max_done, 1)

            def norm(b):
                dve.wait_ge(exp_done, 2 * b + 2)
                link(nc.vector.reciprocal(erec[:, 2 * b:2 * b + 2], esum[:, 2 * b:2 * b + 2]))
                for m in range(2):
                    n = 2 * b + m
                    nc.vector.tensor_scalar(att[:, b % 2, m, :], att[:, b % 2, m, :], erec[:, n:n + 1], None,
                                            ALU.mult).then_inc(norm_done, 1)

            def x1(b):
                dve.wait_ge(xm_done, b + 1)
                pair = slice(2 * b, 2 * b + 2)
                nc.vector.tensor_tensor(rows[:, pair, 0:H], p_xm[:].rearrange("p (t h) -> p t h", t=2),
                                        x_sb[:, pair, :], ALU.add).then_inc(x1_done, 1)

            def s2(b):
                pair = slice(2 * b, 2 * b + 2)
                dve.wait_ge(x1_done, b + 1)
                moments(1, b, lambda n: rows[:, n, 0:H]).then_inc(stat2_done, 1)
                nc.vector.tensor_copy(rows[:, pair, MEAN], mv[:, 1, pair, 0])

            def tk(b):
                dve.wait_ge(rstd2_done, b + 1)
                if b >= 2:
                    dve.wait_ge(tt_done, b - 1)
                for t in range(2):
                    n = 2 * b + t
                    nc.vector.tensor_scalar(tok[:, b % 2, t, :], rows[:, n, 0:H], mv[:, 1, n, 0:1],
                                            rows[:, n, RSTD:RSTD + 1], ALU.subtract, ALU.mult).then_inc(tok_done, 1)

            def wide(v):
                return v[:, :, None].to_broadcast([P, 2, E])

            def route(b):
                pair = slice(2 * b, 2 * b + 2)
                if b == 0:
                    dve.wait_ge(consts, 5)
                dve.wait_ge(lg_done, b + 1)
                link(nc.vector.tensor_copy(logits[:, b, :, :], p_gate[:, 0:2 * E].rearrange("p (t e) -> p t e", t=2)))
                nc.vector.tensor_reduce(lmax[:, pair], logits[:, b, :, :], AX.X, ALU.max).then_inc(lmax_done, 1)
                nc.vector.tensor_reduce(nlmax[:, pair], logits[:, b, :, :], AX.X, ALU.max,
                                        negate=True).then_inc(lmax_done, 1)
                dve.wait_ge(lmax_done, 2 * b + 1)
                for n in range(2 * b, 2 * b + 2):
                    last = nc.vector.scalar_tensor_tensor(val[:, b, n % 2, :], logits[:, b, n % 2, :], lmax[:, n:n + 1],
                                                          descend[:, n % 2, :], ALU.is_equal, ALU.mult)
                link(last)
                link(nc.vector.tensor_reduce(vmax[:, pair], val[:, b, :, :], AX.X, ALU.max))
                nc.vector.tensor_tensor(mask[:, b, :, :], val[:, b, :, :], wide(vmax[:, pair]),
                                        ALU.is_equal).then_inc(mask_done, 1)
                nc.vector.tensor_scalar(expert[:, pair], vmax[:, pair], -1.0, float(E), ALU.mult, ALU.add)

            def place(b):
                pair = slice(2 * b, 2 * b + 2)
                dve.wait_ge(zs_done, 2 * b + 2)
                nc.vector.reciprocal(rows[:, pair, WEIGHT], zs[:, pair])
                dve.wait_ge(mask_done, b + 1)
                dve.wait_ge(rk_done, b + 1)
                for n in range(2 * b, 2 * b + 2):
                    o = 64 + (n % 2) * E
                    last = nc.vector.tensor_tensor_reduce(ranked[:, n, :], p_gate[:, o:o + E], mask[:, b, n % 2, :],
                                                          1.0, 0.0, ALU.mult, ALU.add, rank[:, n:n + 1])
                last.then_inc(rank_read, 1)
                dve.wait_ge(rank_read, b + 1)
                nc.vector.scalar_tensor_tensor(slot[:, pair], rank[:, pair], float(E), expert[:, pair],
                                               ALU.mult, ALU.add).then_inc(slot_done, 1)
                if b + 1 < B:
                    dve.wait_ge(seen_done, b + 1)
                    link(nc.vector.tensor_tensor(seen[:, b + 1, :], seen[:, b, :], mask[:, b, 0, :], ALU.add))
                    nc.vector.tensor_tensor(seen[:, b + 1, :], seen[:, b + 1, :], mask[:, b, 1, :],
                                            ALU.add).then_inc(seen_done, 1)

            st1(0)
            st1(1)
            ln(0)
            st1(2)
            mx(0)
            ln(1)
            ln(2)
            norm(0)
            mx(1)
            st1(3)
            norm(1)
            ln(3)
            x1(0)
            s2(0)
            mx(2)
            tk(0)
            norm(2)
            x1(1)
            s2(1)
            route(0)
            mx(3)
            tk(1)
            place(0)
            norm(3)
            x1(2)
            s2(2)
            route(1)
            tk(2)
            place(1)
            x1(3)
            s2(3)
            route(2)
            tk(3)
            place(2)
            route(3)
            place(3)

            def load_tile(i):
                t = IN_TILES[i]
                if i == 0:
                    dve.wait_ge(got_first, 16)
                elif i == 1:
                    dve.wait_ge(got_rem, 16 * STACKS)
                elif i == 2:
                    dve.wait_ge(got_main, 16)
                if i >= 2:
                    dve.wait_ge(dT_done, i - 1)
                nc.vector.tensor_scalar(stok[:, i % 2, :], got[:, t, 0:H], got[:, t, MEAN:MEAN + 1],
                                        got[:, t, RSTD:RSTD + 1], ALU.subtract, ALU.mult).then_inc(stok_done, 1)

            def load_tileT(i):
                t = IN_TILES[i]
                dve.wait_ge(dT_done, i + 1)
                if t < E:
                    nc.vector.tensor_copy(dispT[:, :, t, 0:P], p_dT[i % 2][:, 0:H].rearrange(
                        "p (c s) -> p c s", c=HC)).then_inc(dT_sb, 1)
                else:
                    first = (t - E) * PER_STACK
                    nc.vector.tensor_copy(dispT[:, :, first:first + PER_STACK, P:CAP], p_dT[i % 2][:, 0:H].rearrange(
                        "p (c j s) -> p c j s", c=HC, j=PER_STACK)).then_inc(dT_sb, 1)

            def out_tile(n):
                t = OUT_TILES[n]
                dve.wait_ge(o_done, n + 1)
                if n >= 2:
                    dve.wait_ge(y_out[n % 2], 16 * (n // 2))
                x1_rows, weight = (got[:, t, 0:H], got[:, t, WEIGHT:WEIGHT + 1])
                nc.vector.scalar_tensor_tensor(y[:, n % 2, :], p_o[n % 2][:, 0:H], weight, x1_rows,
                                               ALU.mult, ALU.add).then_inc(y_done, 1)

            load_tile(0)
            load_tile(1)
            for i in FIRST_INS:
                load_tileT(i)
            load_tile(2)
            load_tile(3)
            outs = iter(range(TILES))
            for s in range(E + 1):
                for i in INS_AT[s]:
                    load_tileT(i)
                    if i + 2 < TILES:
                        load_tile(i + 2)
                if s:
                    out_tile(next(outs))
                if s and s % PER_STACK == 0:
                    out_tile(next(outs))

        @block.tensor
        def _(pe):
            def turn(dst, src, n=P):
                return nc.tensor.transpose(dst, src, ident[0:n, 0:n])

            def mm(dst, lhsT, rhs, k, last):
                return nc.tensor.matmul(dst, lhsT, rhs, start=(k == 0), stop=last)

            def ct(g):
                pe.wait_ge(ctx_here[g], 16)
                if g == 0:
                    pe.wait_ge(wT_sb, 1)
                else:
                    pe.wait_ge(ct_sb, g)
                for n in range(4):
                    last = turn(p_ct[:, n * P:(n + 1) * P], ctx_sb[:, 4 * g + n, :])
                last.then_inc(ct_done, 1)

            def q(g):
                pe.wait_ge(ct_sb, g + 1)
                if g:
                    pe.wait_ge(q_sb, g)
                mm(p_q[:], wT[:, 0:C], ctxT[:, g, :], 0, True).then_inc(q_done, 1)

            def k(g):
                pe.wait_ge(ct_sb, g + 1)
                if g:
                    pe.wait_ge(k_sb, g)
                mm(p_k[:], wT[:, C:2 * C], ctxT[:, g, :], 0, True).then_inc(k_done, 1)

            def en(b):
                g, o = b // 2, (b % 2) * S
                pe.wait_ge(q_sb, g + 1)
                pe.wait_ge(k_sb, g + 1)
                if b >= 2:
                    pe.wait_ge(exp_done, 2 * (b - 1))
                for m in range(2):
                    last = mm(p_en[b % 2][:, m * S:(m + 1) * S], qT[:, g, o + m * P:o + (m + 1) * P],
                              kT[:, g, o:o + S], 0, True)
                last.then_inc(en_done, 1)

            def tl(b):
                pe.wait_ge(ln1_done, 2 * b + 2)
                if b:
                    pe.wait_ge(tl_sb, b)
                for c in range(2):
                    for t in range(2):
                        last = turn(p_tl[:, c * S + t * P:c * S + (t + 1) * P], ln1[:, b % 2, t, c * P:(c + 1) * P])
                last.then_inc(tl_done, 1)

            def at(b):
                pe.wait_ge(norm_done, 2 * b + 2)
                if b:
                    pe.wait_ge(at_sb, b)
                for c in range(2):
                    for m in range(2):
                        last = turn(p_at[:, c * S + m * P:c * S + (m + 1) * P], att[:, b % 2, m, c * P:(c + 1) * P])
                last.then_inc(at_done, 1)

            def xm(b):
                pe.wait_ge(at_sb, b + 1)
                pe.wait_ge(tl_sb, b + 1)
                if b:
                    pe.wait_ge(x1_done, b)
                for t in range(2):
                    for c in range(2):
                        last = mm(p_xm[:, t * H:(t + 1) * H], lnT[:, b % 2, c, t * P:(t + 1) * P],
                                  attT[:, b % 2, c, :], c, c == 1)
                last.then_inc(xm_done, 1)

            def tt(b):
                pe.wait_ge(tok_done, 2 * b + 2)
                if b == 0:
                    pe.wait_ge(gt_sb, 1)
                elif b == 1:
                    pe.wait_ge(k_sb, 2)
                else:
                    pe.wait_ge(tt_sb, b - 1)
                for c in range(HC):
                    for t in range(2):
                        last = turn(p_tt[b % 2][:, c * S + t * P:c * S + (t + 1) * P], tok[:, b % 2, t, c * P:(c + 1) * P])
                last.then_inc(tt_done, 1)

            def gt():
                pe.wait_ge(gate_here, 16)
                pe.wait_ge(ct_sb, 2)
                for c in range(HC):
                    last = turn(p_gt[:, c * E:(c + 1) * E], gate_sb[:, c * P:(c + 1) * P], E)
                last.then_inc(gt_done, 1)

            def lg(b):
                pe.wait_ge(tt_sb, b + 1)
                if b == 0:
                    pe.wait_ge(q_sb, 2)
                else:
                    pe.wait_ge(rank_read, b)
                for t in range(2):
                    for c in range(HC):
                        last = mm(p_gate[:, t * E:(t + 1) * E], tokT[:, b % 2, c, t * P:(t + 1) * P],
                                  gateT[:, c, :], c, c == HC - 1)
                last.then_inc(lg_done, 1)

            def rk(b):
                pe.wait_ge(mask_done, b + 1)
                r = p_gate[:, 64:64 + 2 * E]
                pe.wait_ge(seen_done, b + 1)
                nc.tensor.matmul(r, before[:], mask[:, b, :, :], start=True, stop=False, skip_group_check=True)
                for t in range(2):
                    nc.tensor.matmul(r[:, t * E:(t + 1) * E], ones[:], seen[:, b, :], start=False, stop=False,
                                     skip_group_check=True)
                nc.tensor.matmul(r[:, E:2 * E], ones[:], mask[:, b, 0, :], start=False, stop=True,
                                 skip_group_check=True).then_inc(rk_done, 1)

            def keep_warm(n):
                for _ in range(n):
                    nc.tensor.matmul(p_warm[:, 0:P], ident[:], ident[:], start=True, stop=True)

            pe.wait_ge(ident_done, 1)
            keep_warm(WARM_START)
            pe.wait_ge(wqk_here, 32)
            for w in range(2):
                last = turn(p_wT[:, w * C:(w + 1) * C], wqk[:, w, :])
            last.then_inc(wT_done, 1)
            ct(0)
            q(0)
            k(0)
            ct(1)
            en(0)
            tl(0)
            en(1)
            q(1)
            tl(1)
            at(0)
            k(1)
            xm(0)
            en(2)
            at(1)
            gt()
            tl(2)
            xm(1)
            tt(0)
            at(2)
            lg(0)
            en(3)
            tl(3)
            rk(0)
            xm(2)
            tt(1)
            at(3)
            lg(1)
            xm(3)
            rk(1)
            tt(2)
            lg(2)
            rk(2)
            tt(3)
            lg(3)
            rk(3)

            def dT(i):
                pe.wait_ge(stok_done, i + 1)
                if i >= 2:
                    pe.wait_ge(dT_sb, i - 1)
                for c in range(HC):
                    last = turn(p_dT[i % 2][:, c * P:(c + 1) * P], stok[:, i % 2, c * P:(c + 1) * P])
                last.then_inc(dT_done, 1)

            def mm1(e, then=()):
                pe.wait_ge(wi_here[e], 16)
                pe.wait_ge(dT_sb, max(i for i in range(TILES) if FIRST_USE[i] <= e) + 1)
                for j, (a, z_) in enumerate(GROUPS):
                    if e:
                        pe.wait_ge(gelu_done, NG * (e - 1) + j + 1)
                    for i in range(a, z_):
                        for c in range(HC):
                            last = mm(p_h[j][:, (i - a) * CAP:(i - a + 1) * CAP], wi_sb[:, e, c, i * P:(i + 1) * P],
                                      dispT[:, c, e, :], c, c == HC - 1)
                    last.then_inc(h_done, 1)
                    if j == 1:
                        for i in then:
                            dT(i)

            gelu_rows = [gelu[:, e % RING, :, :] for e in range(E)]

            def bank_free(n):
                if n >= 2:
                    pe.wait_ge(y_done, n - 1)

            def mm2(e, n):
                pe.wait_ge(wo_here[e], 16)
                pe.wait_ge(gelu_done, NG * (e + 1))
                bank_free(n)
                for i in range(IC):
                    last = mm(p_o[n % 2][:, 0:H], gelu_rows[e][:, i, 0:P], wo_sb[:, e, i, :], i, i == IC - 1)
                last.then_inc(o_done, 1)

            def mm2_stack(r, n):
                bank_free(n)
                for i in range(IC):
                    for j in range(PER_STACK):
                        e = r * PER_STACK + j
                        last = mm(p_o[n % 2][j * REM:(j + 1) * REM, 0:H], gelu_rows[e][:, i, P:CAP],
                                  wo_sb[:, e, i, :], i, i == IC - 1)
                last.then_inc(o_done, 1)

            keep_warm(WARM_DISPATCH)
            for i in FIRST_INS:
                dT(i)
            outs = iter(range(TILES))
            for s in range(E + 1):
                if s == 0:
                    mm1(0, then=INS_AT[0])
                elif s < E:
                    for i in INS_AT[s]:
                        dT(i)
                    mm1(s)
                if s:
                    mm2(s - 1, next(outs))
                if s and s % PER_STACK == 0:
                    mm2_stack(s // PER_STACK - 1, next(outs))


_INS = ["x", "ctx_1024", "L0_xattn_Wq", "L0_xattn_bq", "L0_xattn_Wk", "L0_xattn_bk", "L0_ffn_gate_weight",
        "L0_ffn_wi", "L0_ffn_wo"]


def kernel(**inputs):
    import numpy as _np
    import concourse.bacc as _bacc
    from concourse import mybir as _mybir
    from concourse.bass_utils import run_bass_kernel_spmd as _run

    nc = _bacc.Bacc("TRN2", target_bir_lowering=False, num_devices=1)
    arrays, args = {}, []
    for name in _INS:
        a = _np.ascontiguousarray(inputs[name])
        arrays[f"in_{name}"] = a
        args.append(nc.dram_tensor(f"in_{name}", a.shape, _mybir.dt.from_np(a.dtype), kind="ExternalInput").ap())
    args.append(nc.dram_tensor("out_0", (B, S, H), F32, kind="ExternalOutput").ap())
    xattn_moe(nc, *args)
    r = _run(nc, [arrays], core_ids=[0])
    return r.results[0]["out_0"]
```

```python
from contextlib import ExitStack

import concourse.bass as bass
from concourse import mybir

ALU = mybir.AluOpType
ACT = mybir.ActivationFunctionType
AX = mybir.AxisListType
F32 = mybir.dt.float32
BF16 = mybir.dt.bfloat16
I32 = mybir.dt.int32

P = 128
B = 4
S = 256
H = 256
C = 128
E = 8
F = 1024
T = B * S
NT = T // P
CAP = 160
REM = CAP - P
PER_STACK = P // REM
STACKS = E // PER_STACK
HC = H // P
IC = F // P
EPS = 1e-5
ROW = H + 4
MEAN, RSTD, INDEX, WEIGHT = H, H + 1, H + 2, H + 3
NOWHERE = 1 << 20
GROUPS = [(0, 3), (3, 6), (6, 8)]
NG = len(GROUPS)
WIDE = H + 2 * E
HALF = WIDE // 2
WARM_START = 4
WARM_INPUT = 1
WARM_DISPATCH = 1


def xattn_moe(nc, x, ctx_in, wq, bq, wk, bk, gate, wi, wo, out):
    assert CAP == (lambda c: c + c % 2)(int(1.25 * T / E))
    x_v = x.rearrange("b (t p) h -> b p t h", p=P)
    ctx_v = ctx_in.rearrange("(g b) (t p) c -> g p (b t) c", b=2, p=P)
    out_rows = out.rearrange("b s h -> (b s) h")
    out_v = out.rearrange("b (t p) h -> b p t h", p=P)
    wi_v = wi.rearrange("e (k p) i -> e p k i", p=P)
    wo_v = wo.rearrange("e (i p) h -> e p i h", p=P)

    with ExitStack() as stack:
        def sb(name, shape, dt=F32):
            return stack.enter_context(nc.sbuf_tensor(name, shape, dt))

        def sem(name):
            return stack.enter_context(nc.semaphore(name))

        bank = [stack.enter_context(nc.psum_tensor(f"bank{i}", [P, 512], F32)) for i in range(8)]

        slots_dram = nc.dram_tensor("slots_dram", [E * CAP, ROW], F32, kind="Internal").ap()
        by_rank = slots_dram.rearrange("(c e) r -> c e r", e=E)

        wi_sb = sb("wi_sb", [P, E, HC, F])
        wo_sb = sb("wo_sb", [P, E, IC, H])
        RING = PER_STACK + 1
        shared = sb("shared", [P, HC * E * CAP + RING * IC * CAP + P * 2])

        def part(at, size, pattern, **sizes):
            assert at + size <= shared.shape[1]
            return shared[:, at:at + size].rearrange(f"p ({pattern}) -> p {pattern}", **sizes)

        x_sb = part(0, NT * H, "n h", n=NT)
        ctx_sb = part(2048, NT * C, "n c", n=NT)
        ctxT = part(3072, 4 * S, "g s", g=2)
        qT = part(4096, 4 * S, "g s", g=2)
        kT = part(5120, 4 * S, "g s", g=2)
        ln1 = part(6144, 4 * H, "b t h", b=2, t=2)
        att = part(7168, 4 * S, "b t s", b=2, t=2)
        lnT = part(8192, 4 * S, "b t s", b=2, t=2)
        onehot = part(2560, NT * CAP, "n s", n=NT)
        tok = part(4096, NT * H, "n h", n=NT)
        dispT = part(0, HC * E * CAP, "k e s", k=HC, e=E)
        gelu = part(HC * E * CAP, RING * IC * CAP, "b i s", b=RING, i=IC)
        rows = sb("rows", [P, NT, ROW])
        wqk = sb("wqk", [P, 2, C])
        gate_sb = sb("gate_sb", [E, H])
        bias = sb("bias", [P, 2])
        wT = sb("wT", [P, 2 * C])
        gate_mv = sb("gate_mv", [E, 8])
        ident = sb("ident", [P, P])
        before = sb("before", [P, P], BF16)
        ones = sb("ones", [P, P], BF16)
        attended = sb("attended", [P, 2, HC, WIDE])
        gateT = attended[:, 0, :, 0:E]
        stok = sb("stok", [P, 2, H])
        y = sb("y", [P, 2, H])
        turner = sb("turner", [P, 2, WIDE])
        stats = sb("stats", [P, 2, NT, 6])
        mv = sb("mv", [P, NT, 2])
        rstd1 = sb("rstd1", [P, NT])
        std1 = sb("std1", [P, NT])
        shift1 = sb("shift1", [P, NT])
        minus_half = sb("minus_half", [P, 2])
        nmax = sb("nmax", [P, NT])
        esum = sb("esum", [P, NT])
        erec = sb("erec", [P, NT])
        descend = sb("descend", [P, 2, E])
        logits = sb("logits", [P, B, 2, E])
        lmax = sb("lmax", [P, NT])
        below = sb("below", [P, B, 2, E])
        ez = sb("ez", [P, NT, E])
        zs = sb("zs", [P, NT])
        val = sb("val", [P, B, 2, E])
        vmax = sb("vmax", [P, NT])
        mask = sb("mask", [P, B, 2, E], BF16)
        ranked = sb("ranked", [P, NT, E])
        rank = sb("rank", [P, NT])
        slot = sb("slot", [P, NT], I32)
        slot_f = sb("slot_f", [P, NT])
        shift2 = sb("shift2", [P, NT])
        first_slots = sb("first_slots", [P, CAP])
        fill = sb("fill", [P, ROW])
        got = sb("got", [P, E + STACKS, ROW])

        p_ct, p_gt = bank[0], bank[0]
        p_wT = bank[4]
        p_q, p_rank = bank[1], bank[1]
        p_k = bank[2]
        p_en = [bank[3], bank[7]]
        p_tl, p_at, p_xm = bank[4], [bank[5], bank[0]], [bank[6], bank[2]]
        p_h = [bank[2], bank[3], bank[4]]
        p_disp = bank[3]
        p_dT = [bank[0], bank[1]]
        p_o = [bank[5], bank[6]]
        p_warm = bank[7]

        x_in = [sem(f"x_in{b}") for b in range(B)]
        ctx_here = [sem(f"ctx_here{g}") for g in range(2)]
        wqk_here = sem("wqk_here")
        bias_here = sem("bias_here")
        gate_here = sem("gate_here")
        wi_here = [sem(f"wi_here{e}") for e in range(E)]
        wo_here = [sem(f"wo_here{e}") for e in range(E)]
        zeroed = sem("zeroed")
        ident_done = sem("ident_done")
        consts = sem("consts")
        fill_done = sem("fill_done")
        filled = sem("filled")
        wT_done, wT_sb = sem("wT_done"), sem("wT_sb")
        gt_done, gt_sb = sem("gt_done"), sem("gt_sb")
        ct_done, ct_sb = sem("ct_done"), sem("ct_sb")
        q_done, q_sb = sem("q_done"), sem("q_sb")
        k_done, k_sb = sem("k_done"), sem("k_sb")
        stat1_done, rstd1_done, ln1_done = sem("stat1_done"), sem("rstd1_done"), sem("ln1_done")
        en_done, max_done, exp_done = sem("en_done"), sem("max_done"), sem("exp_done")
        tl_done, tl_sb = sem("tl_done"), sem("tl_sb")
        at_done, at_sb = sem("at_done"), sem("at_sb")
        shift_done, erec_done = sem("shift_done"), sem("erec_done")
        turner_done, scaled_done = sem("turner_done"), sem("scaled_done")
        xm_done, x1_done = sem("xm_done"), sem("x1_done")
        stat2_done, rstd2_done = sem("stat2_done"), sem("rstd2_done")
        scaled_logits, logits_done, lmax_done = sem("scaled_logits"), sem("logits_done"), sem("lmax_done")
        veps1_done, veps2_done = sem("veps1_done"), sem("veps2_done")
        bn1_done, bn2_done = sem("bn1_done"), sem("bn2_done")
        val_done, vmax_done = sem("val_done"), sem("vmax_done")
        below_done, zs_done, weight_done = sem("below_done"), sem("zs_done"), sem("weight_done")
        mask_done, rk_done, slot_done = sem("mask_done"), sem("rk_done"), sem("slot_done")
        rank_read = sem("rank_read")
        centred = sem("centred")
        dve_step = sem("dve_step")
        x1_out = sem("x1_out")
        scattered = sem("scattered")
        got_zero, got_one, got_main = sem("got_zero"), sem("got_one"), sem("got_main")
        got_rem = [sem(f"got_rem{r}") for r in range(STACKS)]
        stok_done, dT_done, dT_sb = sem("stok_done"), sem("dT_done"), sem("dT_sb")
        shift2_done, tok_done, onehot_done = sem("shift2_done"), sem("tok_done"), sem("onehot_done")
        disp_done, disp_sb = sem("disp_done"), sem("disp_sb")
        h_done, gelu_done = sem("h_done"), sem("gelu_done")
        o_done, y_done = sem("o_done"), sem("y_done")
        y_out = [sem("y_out0"), sem("y_out1")]

        IN_TILES = [1, E] + list(range(2, PER_STACK)) + [E + 1] + list(range(PER_STACK, E))
        OUT_TILES = list(range(PER_STACK)) + [E] + list(range(PER_STACK, E)) + [E + 1]
        INS, OUTS = len(IN_TILES), len(OUT_TILES)
        FIRST_USE = [max(1, t if t < E else (t - E) * PER_STACK) for t in IN_TILES]
        INS_AT = [[i for i in range(INS) if FIRST_USE[i] == s + 1] for s in range(E + 1)]

        def tokens_of(pairs, b):
            return pairs[:, b // 2, (b % 2) * S:(b % 2 + 1) * S]

        block = stack.enter_context(nc.Block())

        @block.sync
        def _(sp):
            def last_slots(r):
                first = r * PER_STACK
                sp.dma_start(got[:, E + r, :],
                             by_rank[P:CAP, first:first + PER_STACK, :].rearrange("q j w -> j q w")
                             ).then_inc(got_rem[r], 16)

            def weights(e):
                sp.dma_start(wi_sb[:, e, :, :], wi_v[e]).then_inc(wi_here[e], 16)
                sp.dma_start(wo_sb[:, e, :, :], wo_v[e]).then_inc(wo_here[e], 16)

            sp.dma_start(ctx_sb[:, 0:4, :], ctx_v[0]).then_inc(ctx_here[0], 16)
            sp.dma_start(wqk[:, 0, :], wq).then_inc(wqk_here, 16)
            sp.dma_start(x_sb[:, 0:2, :], x_v[0]).then_inc(x_in[0], 16)
            sp.dma_start(x_sb[:, 2:4, :], x_v[1]).then_inc(x_in[1], 16)
            sp.dma_start(ctx_sb[:, 4:8, :], ctx_v[1]).then_inc(ctx_here[1], 16)
            sp.dma_start(x_sb[:, 4:6, :], x_v[2]).then_inc(x_in[2], 16)
            sp.dma_start(x_sb[:, 6:8, :], x_v[3]).then_inc(x_in[3], 16)
            sp.wait_ge(fill_done, 2)
            sp.dma_start(slots_dram.rearrange("(n p) r -> p n r", p=P),
                         fill[:, None, :].to_broadcast([P, E * CAP // P, ROW])).then_inc(filled, 16)
            weights(0)
            weights(1)
            sp.wait_ge(x1_done, 2)
            weights(2)

            sp.wait_ge(scattered, 16 * NT)
            sp.dma_start(got[:, 1, :], by_rank[0:P, 1, :]).then_inc(got_one, 16)
            last_slots(0)
            sp.dma_start(got[:, 0, :], by_rank[0:P, 0, :]).then_inc(got_zero, 16)
            sp.dma_start(got[:, 2:E, :], by_rank[0:P, 2:E, :]).then_inc(got_main, 16)
            last_slots(1)
            for b in range(B):
                sp.dma_start(out_v[b], rows[:, 2 * b:2 * b + 2, 0:H]).then_inc(x1_out, 16)
            weights(3)
            weights(4)
            for e in range(5, E):
                sp.wait_ge(o_done, e - 3)
                weights(e)

        @block.gpsimd
        def _(pool):
            nc.gpsimd.memset(ident[:], 0.0).then_inc(zeroed, 1)
            pool.wait_ge(zeroed, 1)
            nc.gpsimd.affine_select(out=ident[:], in_=ident[:], compare_op=ALU.not_equal, fill=1.0, base=0,
                                    pattern=[[-1, P]], channel_multiplier=1).then_inc(ident_done, 1)
            nc.gpsimd.memset(fill[:], 0.0).then_inc(fill_done, 1)
            pool.wait_ge(fill_done, 1)
            nc.gpsimd.memset(fill[:, INDEX:INDEX + 1].bitcast(I32), NOWHERE).then_inc(fill_done, 1)

            nc.gpsimd.memset(minus_half[:], -0.5).then_inc(consts, 1)
            pool.wait_ge(consts, 1)

            def first_rstd(b):
                pool.wait_ge(veps1_done, b + 1)
                pair = slice(2 * b, 2 * b + 2)
                nc.gpsimd.tensor_tensor(rstd1[:, pair], mv[:, pair, 1], minus_half[:], ALU.pow).then_inc(rstd1_done, 1)

            def second_rstd(b):
                pool.wait_ge(veps2_done, b + 1)
                pair = slice(2 * b, 2 * b + 2)
                nc.gpsimd.tensor_tensor(rows[:, pair, RSTD], rows[:, pair, RSTD], minus_half[:],
                                        ALU.pow).then_inc(rstd2_done, 1)

            def scatter(b):
                pool.wait_ge(slot_done, 2 * b + 2)
                pool.wait_ge(weight_done, b + 1)
                if b == 0:
                    pool.wait_ge(filled, 16)
                for n in range(2 * b, 2 * b + 2):
                    nc.gpsimd.indirect_dma_start(
                        slots_dram, bass.IndirectOffsetOnAxis(ap=slot[:, n:n + 1], axis=0), rows[:, n, :], None,
                        bounds_check=E * CAP - 1, oob_is_err=False).then_inc(scattered, 16)

            nc.gpsimd.memset(before[:], 1.0).then_inc(zeroed, 1)
            nc.gpsimd.memset(ones[:], 1.0).then_inc(consts, 1)
            pool.wait_ge(zeroed, 2)
            nc.gpsimd.affine_select(out=before[:], in_=before[:], compare_op=ALU.is_gt, fill=0.0, base=0,
                                    pattern=[[1, P]], channel_multiplier=-1).then_inc(consts, 1)
            nc.gpsimd.iota(descend[:], pattern=[[0, 2], [-1, E]], base=E, channel_multiplier=0,
                           allow_small_or_imprecise_dtypes=True).then_inc(consts, 1)
            nc.gpsimd.iota(first_slots[:], pattern=[[E, CAP]], base=0, channel_multiplier=0,
                           allow_small_or_imprecise_dtypes=True).then_inc(consts, 1)
            nc.gpsimd.iota(rows[:, :, INDEX].bitcast(I32), pattern=[[P, NT]], base=0,
                           channel_multiplier=1).then_inc(consts, 1)
            first_rstd(0)
            first_rstd(1)
            first_rstd(2)
            first_rstd(3)
            second_rstd(0)
            second_rstd(1)
            scatter(0)
            second_rstd(2)
            scatter(1)
            second_rstd(3)
            scatter(2)
            scatter(3)

            pool.wait_ge(x1_out, 16 * B)
            for n, t in enumerate(OUT_TILES):
                pool.wait_ge(y_done, n + 1)
                nc.gpsimd.indirect_dma_start(
                    out_rows, bass.IndirectOffsetOnAxis(ap=got[:, t, INDEX:INDEX + 1].bitcast(I32), axis=0),
                    y[:, n % 2, :], None, bounds_check=T - 1, oob_is_err=False).then_inc(y_out[n % 2], 16)
            for n in range(2):
                pool.wait_ge(y_out[n], 16 * (len(OUT_TILES) // 2))

        @block.scalar
        def _(act):
            act.dma_start(wqk[:, 1, :], wk).then_inc(wqk_here, 16)
            nc.scalar.preload_act_table(ACT.Exp)
            act.dma_start(gate_sb[:], gate).then_inc(gate_here, 16)
            act.dma_start(bias[:, 0:1], bq.rearrange("(d a) -> d a", a=1)).then_inc(bias_here, 16)
            act.dma_start(bias[:, 1:2], bk.rearrange("(d a) -> d a", a=1)).then_inc(bias_here, 16)

            def copy(dst, src):
                return nc.scalar.activation(dst, src, ACT.Copy)

            def ct(g):
                act.wait_ge(ct_done, g + 1)
                copy(ctxT[:, g, :], p_ct[:]).then_inc(ct_sb, 1)

            def q(b):
                act.wait_ge(q_done, b + 1)
                if b == 0:
                    act.wait_ge(bias_here, 32)
                nc.scalar.activation(tokens_of(qT, b), p_q[:, 0:S], ACT.Identity, bias=bias[:, 0:1]).then_inc(q_sb, 1)

            def k(b):
                act.wait_ge(k_done, b + 1)
                nc.scalar.activation(tokens_of(kT, b), p_k[:, 0:S], ACT.Identity, bias=bias[:, 1:2]).then_inc(k_sb, 1)

            def exp(b):
                act.wait_ge(max_done, b + 1)
                if b >= 2:
                    act.wait_ge(at_done, HC * (b - 1))
                for m in range(2):
                    n = 2 * b + m
                    nc.scalar.activation(att[:, b % 2, m, :], p_en[b % 2][:, m * S:(m + 1) * S], ACT.Exp,
                                         bias=nmax[:, n:n + 1], accum_out=esum[:, n:n + 1]).then_inc(exp_done, 1)

            def ln(b):
                act.wait_ge(shift_done, 2 * b + 1)
                if b >= 2:
                    act.wait_ge(tl_done, b - 1)
                for t in range(2):
                    n = 2 * b + t
                    nc.scalar.activation(ln1[:, b % 2, t, :], x_sb[:, n, :], ACT.Identity, bias=shift1[:, n:n + 1],
                                         scale=rstd1[:, n:n + 1]).then_inc(ln1_done, 1)

            def turn_by(b):
                act.wait_ge(erec_done, b + 1)
                if b >= 2:
                    act.wait_ge(at_done, HC * (b - 1))
                for m in range(2):
                    n = 2 * b + m
                    o = m * (P + 2 * E)
                    nc.scalar.activation(turner[:, b % 2, o:o + P], ident[:], ACT.Copy,
                                         scale=erec[:, n:n + 1]).then_inc(turner_done, 1)

            def tl(b):
                act.wait_ge(tl_done, b + 1)
                if b >= 2:
                    act.wait_ge(xm_done, 2 * (b - 1))
                copy(lnT[:, b % 2, :, :], p_tl[:]).then_inc(tl_sb, 1)

            def at(b):
                if b >= 2:
                    act.wait_ge(xm_done, 2 * (b - 1))
                for c in range(HC):
                    act.wait_ge(at_done, HC * b + c + 1)
                    copy(attended[:, b % 2, c, E:WIDE], p_at[c][:, E:WIDE]).then_inc(at_sb, 1)

            def expz(b):
                act.wait_ge(below_done, b + 1)
                act.wait_ge(rstd2_done, b + 1)
                for n in range(2 * b, 2 * b + 2):
                    nc.scalar.activation(ez[:, n, :], below[:, b, n % 2, :], ACT.Exp, scale=rows[:, n, RSTD:RSTD + 1],
                                         accum_out=zs[:, n:n + 1]).then_inc(zs_done, 1)

            def tokens(b):
                act.wait_ge(shift2_done, b + 1)
                if b == 0:
                    act.wait_ge(en_done, B)
                for n in range(2 * b, 2 * b + 2):
                    nc.scalar.activation(tok[:, n, :], rows[:, n, 0:H], ACT.Identity, bias=shift2[:, n:n + 1],
                                         scale=rows[:, n, RSTD:RSTD + 1]).then_inc(tok_done, 1)

            def gt():
                act.wait_ge(gt_done, 1)
                copy(attended[:, :, :, 0:E], p_gt[:, 0:HC * E].rearrange("p (c e) -> p c e", c=HC)[:, None, :, :]
                     .to_broadcast([P, 2, HC, E])).then_inc(gt_sb, 1)

            ct(0)
            q(0)
            k(0)
            ct(1)
            q(1)
            ln(0)
            k(1)
            exp(0)
            gt()
            k(2)
            q(2)
            turn_by(0)
            tl(0)
            exp(1)
            k(3)
            at(0)
            turn_by(1)
            exp(2)
            ln(1)
            q(3)
            turn_by(2)
            at(1)
            tl(1)
            ln(2)
            exp(3)
            at(2)
            tl(2)
            turn_by(3)
            ln(3)
            expz(0)
            tokens(0)
            at(3)
            tl(3)
            expz(1)
            tokens(1)
            expz(2)
            tokens(2)
            tokens(3)
            expz(3)
            nc.scalar.preload_act_table(ACT.Gelu)


            for e in range(E):
                if e >= RING:
                    act.wait_ge(o_done, PER_STACK + 1)
                for j, (a, z) in enumerate(GROUPS):
                    act.wait_ge(h_done, NG * e + j + 1)
                    nc.scalar.activation(gelu[:, e % RING, a:z, :], p_h[j][:, 0:(z - a) * CAP],
                                         ACT.Gelu).then_inc(gelu_done, 1)

        @block.vector
        def _(dve):
            steps = [0]

            def link(ins):
                steps[0] += 1
                ins.then_inc(dve_step, 1)
                dve.wait_ge(dve_step, steps[0])

            def centre():
                dve.wait_ge(gate_here, 16)
                link(nc.vector.bn_stats(gate_mv[:, 0:6], gate_sb[:]))
                link(nc.vector.bn_aggr(gate_mv[:, 6:8], gate_mv[:, 0:6]))
                nc.vector.tensor_scalar(gate_sb[:], gate_sb[:], gate_mv[:, 6:7], None,
                                        ALU.subtract).then_inc(centred, 1)

            def bn1(n):
                dve.wait_ge(x_in[n // 2], 16)
                nc.vector.bn_stats(stats[:, 0, n, :], x_sb[:, n, :]).then_inc(bn1_done, 1)

            def st1(b):
                dve.wait_ge(bn1_done, 2 * b + 2)
                for n in range(2 * b, 2 * b + 2):
                    last = nc.vector.bn_aggr(mv[:, n, :], stats[:, 0, n, :])
                last.then_inc(stat1_done, 1)

            def veps1(b):
                pair = slice(2 * b, 2 * b + 2)
                dve.wait_ge(stat1_done, b + 1)
                nc.vector.tensor_scalar(mv[:, pair, 1], mv[:, pair, 1], EPS, None, ALU.add).then_inc(veps1_done, 1)

            def shift(b):
                pair = slice(2 * b, 2 * b + 2)
                dve.wait_ge(rstd1_done, b + 1)
                nc.vector.scalar_tensor_tensor(shift1[:, pair], mv[:, pair, 0], -1.0, rstd1[:, pair],
                                               ALU.mult, ALU.mult).then_inc(shift_done, 1)
                nc.vector.tensor_tensor(std1[:, pair], mv[:, pair, 1], rstd1[:, pair], ALU.mult).then_inc(shift_done, 1)

            def mx(b):
                dve.wait_ge(en_done, b + 1)
                nc.vector.tensor_reduce(nmax[:, 2 * b:2 * b + 2], p_en[b % 2][:].rearrange("p (m s) -> p m s", m=2),
                                        AX.X, ALU.max, negate=True).then_inc(max_done, 1)

            def recip(b):
                pair = slice(2 * b, 2 * b + 2)
                dve.wait_ge(exp_done, 2 * b + 2)
                nc.vector.reciprocal(erec[:, pair], esum[:, pair]).then_inc(erec_done, 1)

            def scales(b):
                pair = slice(2 * b, 2 * b + 2)
                if b == 0:
                    dve.wait_ge(gt_sb, 1)
                if b >= 2:
                    dve.wait_ge(at_done, HC * (b - 1))
                dve.wait_ge(erec_done, b + 1)
                nc.vector.tensor_tensor(turner[:, b % 2, P:P + 2 * E].rearrange("p (m e) -> p m e", m=2), gateT,
                                        wide(erec[:, pair]), ALU.mult).then_inc(scaled_done, 1)

            def halves(v):
                return v.rearrange("p (m w) -> p m w", m=2)

            def part1(n):
                dve.wait_ge(xm_done, n + 1)
                dve.wait_ge(shift_done, 2 * (n // 2) + 2)
                nc.vector.tensor_scalar(logits[:, n // 2, n % 2, :], p_xm[n % 2][:, 0:E], std1[:, n:n + 1], None,
                                        ALU.mult).then_inc(scaled_logits, 1)

            def part2(n):
                dve.wait_ge(scaled_logits, n + 1)
                nc.vector.tensor_tensor(logits[:, n // 2, n % 2, :], logits[:, n // 2, n % 2, :],
                                        p_xm[n % 2][:, HALF:HALF + E], ALU.add).then_inc(logits_done, 1)

            def x1(n):
                dve.wait_ge(xm_done, n + 1)
                nc.vector.tensor_tensor(halves(rows[:, n, 0:H]), halves(p_xm[n % 2][:, 0:WIDE])[:, :, E:HALF],
                                        halves(x_sb[:, n, :]), ALU.add).then_inc(x1_done, 1)

            def bn2(n):
                dve.wait_ge(x1_done, n + 1)
                nc.vector.bn_stats(stats[:, 1, n, :], rows[:, n, 0:H]).then_inc(bn2_done, 1)

            def st2(b):
                dve.wait_ge(bn2_done, 2 * b + 2)
                for n in range(2 * b, 2 * b + 2):
                    last = nc.vector.bn_aggr(rows[:, n, MEAN:RSTD + 1], stats[:, 1, n, :])
                last.then_inc(stat2_done, 1)

            def wide(v):
                return v[:, :, None].to_broadcast([P, 2, E])

            def veps2(b):
                pair = slice(2 * b, 2 * b + 2)
                dve.wait_ge(stat2_done, b + 1)
                nc.vector.tensor_scalar(rows[:, pair, RSTD], rows[:, pair, RSTD], EPS, None,
                                        ALU.add).then_inc(veps2_done, 1)

            def largest(b):
                dve.wait_ge(logits_done, 2 * b + 2)
                nc.vector.tensor_reduce(lmax[:, 2 * b:2 * b + 2], logits[:, b, :, :], AX.X, ALU.max).then_inc(lmax_done, 1)

            def less(b):
                dve.wait_ge(lmax_done, b + 1)
                nc.vector.tensor_tensor(below[:, b, :, :], logits[:, b, :, :], wide(lmax[:, 2 * b:2 * b + 2]),
                                        ALU.subtract).then_inc(below_done, 1)

            def value(b):
                if b == 0:
                    dve.wait_ge(consts, 6)
                dve.wait_ge(below_done, b + 1)
                nc.vector.scalar_tensor_tensor(val[:, b, :, :], below[:, b, :, :], 0.0, descend[:], ALU.is_equal,
                                               ALU.mult).then_inc(val_done, 1)

            def first(b):
                dve.wait_ge(val_done, b + 1)
                nc.vector.tensor_reduce(vmax[:, 2 * b:2 * b + 2], val[:, b, :, :], AX.X, ALU.max).then_inc(vmax_done, 1)

            def chosen(b):
                dve.wait_ge(vmax_done, b + 1)
                nc.vector.tensor_tensor(mask[:, b, :, :], val[:, b, :, :], wide(vmax[:, 2 * b:2 * b + 2]),
                                        ALU.is_equal).then_inc(mask_done, 1)

            def weight(b):
                pair = slice(2 * b, 2 * b + 2)
                dve.wait_ge(zs_done, 2 * b + 2)
                nc.vector.reciprocal(rows[:, pair, WEIGHT], zs[:, pair]).then_inc(weight_done, 1)

            def shifted(b):
                pair = slice(2 * b, 2 * b + 2)
                dve.wait_ge(rstd2_done, b + 1)
                nc.vector.scalar_tensor_tensor(shift2[:, pair], rows[:, pair, MEAN], -1.0, rows[:, pair, RSTD],
                                               ALU.mult, ALU.mult).then_inc(shift2_done, 1)

            def ranks(b):
                dve.wait_ge(mask_done, b + 1)
                dve.wait_ge(rk_done, b + 1)
                for n in range(2 * b, 2 * b + 2):
                    o = (n % 2) * E
                    last = nc.vector.tensor_tensor_reduce(ranked[:, n, :], p_rank[:, o:o + E], mask[:, b, n % 2, :],
                                                          1.0, 1.0, ALU.mult, ALU.add, rank[:, n:n + 1])
                last.then_inc(rank_read, 1)

            def place(b):
                pair = slice(2 * b, 2 * b + 2)
                dve.wait_ge(rank_read, b + 1)
                nc.vector.scalar_tensor_tensor(slot_f[:, pair], rank[:, pair], float(E), vmax[:, pair],
                                               ALU.mult, ALU.subtract).then_inc(slot_done, 1)
                nc.vector.scalar_tensor_tensor(slot[:, pair], rank[:, pair], float(E), vmax[:, pair],
                                               ALU.mult, ALU.subtract).then_inc(slot_done, 1)

            def pick(n):
                dve.wait_ge(slot_done, 2 * (n // 2) + 1)
                if n == 0:
                    dve.wait_ge(k_done, B)
                    dve.wait_ge(q_done, B)
                nc.vector.tensor_scalar(onehot[:, n, :], first_slots[:], slot_f[:, n:n + 1], None,
                                        ALU.is_equal).then_inc(onehot_done, 1)

            def weightsT():
                dve.wait_ge(wT_done, 1)
                nc.vector.tensor_copy(wT[:], p_wT[:, 0:2 * C]).then_inc(wT_sb, 1)

            weightsT()
            centre()
            bn1(0)
            bn1(1)
            bn1(2)
            st1(0)
            bn1(3)
            veps1(0)
            st1(1)
            veps1(1)
            bn1(4)
            bn1(5)
            shift(0)
            st1(2)
            bn1(6)
            bn1(7)
            mx(0)
            st1(3)
            veps1(2)
            shift(1)
            veps1(3)
            shift(2)
            recip(0)
            scales(0)
            shift(3)
            mx(1)
            mx(2)
            recip(1)
            scales(1)
            part1(0)
            x1(0)
            recip(2)
            part2(0)
            bn2(0)
            scales(2)
            x1(1)
            part1(1)
            bn2(1)
            part2(1)
            st2(0)
            largest(0)
            veps2(0)
            less(0)
            mx(3)
            value(0)
            first(0)
            shifted(0)
            chosen(0)
            part1(2)
            x1(2)
            part2(2)
            recip(3)
            ranks(0)
            scales(3)
            bn2(2)
            place(0)
            x1(3)
            part1(3)
            bn2(3)
            part2(3)
            pick(0)
            st2(1)
            largest(1)
            part1(4)
            veps2(1)
            less(1)
            x1(4)
            weight(0)
            value(1)
            bn2(4)
            first(1)
            shifted(1)
            part2(4)
            chosen(1)
            x1(5)
            part1(5)
            bn2(5)
            part2(5)
            pick(1)
            largest(2)
            st2(2)
            less(2)
            ranks(1)
            veps2(2)
            value(2)
            place(1)
            first(2)
            weight(1)
            pick(2)
            x1(6)
            part1(6)
            bn2(6)
            pick(3)
            x1(7)
            part2(6)
            weight(2)
            bn2(7)
            part1(7)
            st2(3)
            part2(7)
            chosen(2)
            veps2(3)
            largest(3)
            shifted(2)
            less(3)
            value(3)
            ranks(2)
            first(3)
            place(2)
            chosen(3)
            shifted(3)
            pick(4)
            pick(5)
            ranks(3)
            place(3)
            pick(6)
            pick(7)
            weight(3)

            dve.wait_ge(disp_done, 1)
            nc.vector.tensor_copy(dispT[:, :, 0, :], p_disp[:, 0:HC * CAP].rearrange("p (c s) -> p c s", c=HC)
                                  ).then_inc(disp_sb, 1)

            def load_tile(i):
                t = IN_TILES[i]
                if i == 0:
                    dve.wait_ge(got_one, 16)
                elif i == 1:
                    dve.wait_ge(got_rem[0], 16)
                elif i == 2:
                    dve.wait_ge(got_main, 16)
                elif t == E + 1:
                    dve.wait_ge(got_rem[1], 16)
                if i >= 2:
                    dve.wait_ge(dT_done, i - 1)
                nc.vector.tensor_scalar(stok[:, i % 2, :], got[:, t, 0:H], got[:, t, MEAN:MEAN + 1],
                                        got[:, t, RSTD:RSTD + 1], ALU.subtract, ALU.mult).then_inc(stok_done, 1)

            def load_tileT(i):
                t = IN_TILES[i]
                dve.wait_ge(dT_done, i + 1)
                if t < E:
                    nc.vector.tensor_copy(dispT[:, :, t, 0:P], p_dT[i % 2][:, 0:H].rearrange(
                        "p (c s) -> p c s", c=HC)).then_inc(dT_sb, 1)
                else:
                    first = max(1, (t - E) * PER_STACK)
                    end = (t - E + 1) * PER_STACK
                    nc.vector.tensor_copy(dispT[:, :, first:end, P:CAP], p_dT[i % 2][:, 0:H].rearrange(
                        "p (c j s) -> p c j s", c=HC, j=PER_STACK)[:, :, first - end + PER_STACK:, :]).then_inc(dT_sb, 1)

            def out_tile(n):
                t = OUT_TILES[n]
                if n == 0:
                    dve.wait_ge(got_zero, 16)
                dve.wait_ge(o_done, n + 1)
                if n >= 2:
                    dve.wait_ge(y_out[n % 2], 16 * (n // 2))
                x1_rows, weight = (got[:, t, 0:H], got[:, t, WEIGHT:WEIGHT + 1])
                nc.vector.scalar_tensor_tensor(y[:, n % 2, :], p_o[n % 2][:, 0:H], weight, x1_rows,
                                               ALU.mult, ALU.add).then_inc(y_done, 1)

            load_tile(0)
            load_tile(1)
            outs = iter(range(OUTS))
            for s in range(E + 1):
                for i in INS_AT[s]:
                    load_tileT(i)
                for i in INS_AT[s]:
                    if i + 2 < INS:
                        load_tile(i + 2)
                if s != 1:
                    out_tile(next(outs))
                if s and s % PER_STACK == 0:
                    out_tile(next(outs))

        @block.tensor
        def _(pe):
            def turn(dst, src, n=P):
                return nc.tensor.transpose(dst, src, ident[0:n, 0:n])

            def mm(dst, lhsT, rhs, k, last):
                return nc.tensor.matmul(dst, lhsT, rhs, start=(k == 0), stop=last)

            def disp(n):
                pe.wait_ge(tok_done, n + 1)
                pe.wait_ge(onehot_done, n + 1)
                if n == 0:
                    pe.wait_ge(exp_done, 2 * (B - 1))
                for c in range(HC):
                    last = nc.tensor.matmul(p_disp[:, c * CAP:(c + 1) * CAP], tok[:, n, c * P:(c + 1) * P],
                                            onehot[:, n, :], start=(n == 0 and c == 0), stop=(n == NT - 1),
                                            skip_group_check=True)
                if n == NT - 1:
                    last.then_inc(disp_done, 1)

            def keep_warm(n):
                for _ in range(n):
                    nc.tensor.matmul(p_warm[:, 0:P], ident[:], ident[:], start=True, stop=True)

            def ct(g):
                pe.wait_ge(ctx_here[g], 16)
                if g:
                    pe.wait_ge(ct_sb, g)
                for n in range(4):
                    last = turn(p_ct[:, n * P:(n + 1) * P], ctx_sb[:, 4 * g + n, :])
                last.then_inc(ct_done, 1)

            def q(b):
                pe.wait_ge(ct_sb, b // 2 + 1)
                if b == 0:
                    pe.wait_ge(wT_sb, 1)
                else:
                    pe.wait_ge(q_sb, b)
                mm(p_q[:, 0:S], wT[:, 0:C], tokens_of(ctxT, b), 0, True).then_inc(q_done, 1)

            def k(b):
                pe.wait_ge(ct_sb, b // 2 + 1)
                if b:
                    pe.wait_ge(k_sb, b)
                mm(p_k[:, 0:S], wT[:, C:2 * C], tokens_of(ctxT, b), 0, True).then_inc(k_done, 1)

            def en(b):
                g, o = b // 2, (b % 2) * S
                pe.wait_ge(q_sb, b + 1)
                pe.wait_ge(k_sb, b + 1)
                if b >= 2:
                    pe.wait_ge(exp_done, 2 * (b - 1))
                for m in range(2):
                    last = mm(p_en[b % 2][:, m * S:(m + 1) * S], qT[:, g, o + m * P:o + (m + 1) * P],
                              kT[:, g, o:o + S], 0, True)
                last.then_inc(en_done, 1)

            def tl(b):
                pe.wait_ge(ln1_done, 2 * b + 2)
                if b:
                    pe.wait_ge(tl_sb, b)
                for c in range(2):
                    for t in range(2):
                        last = turn(p_tl[:, c * S + t * P:c * S + (t + 1) * P], ln1[:, b % 2, t, c * P:(c + 1) * P])
                last.then_inc(tl_done, 1)

            def at(b):
                pe.wait_ge(turner_done, 2 * b + 2)
                pe.wait_ge(scaled_done, b + 1)
                if b == 0:
                    pe.wait_ge(gt_sb, 1)
                for c in range(HC):
                    if b:
                        pe.wait_ge(at_sb, HC * (b - 1) + c + 1)
                    for m in range(2):
                        o = m * HALF
                        last = nc.tensor.matmul(p_at[c][:, E + m * P:E + m * P + HALF], att[:, b % 2, m, c * P:(c + 1) * P],
                                                turner[:, b % 2, o:o + HALF], start=(m == 0), stop=(m == 1),
                                                skip_group_check=True)
                    last.then_inc(at_done, 1)

            def xm(n):
                b, t = n // 2, n % 2
                pe.wait_ge(at_sb, HC * (b + 1))
                pe.wait_ge(tl_sb, b + 1)
                if n >= 2:
                    pe.wait_ge(logits_done, n - 1)
                    pe.wait_ge(x1_done, n - 1)
                elif n == 1:
                    pe.wait_ge(k_sb, B)
                for c in range(2):
                    last = mm(p_xm[t][:, 0:WIDE], lnT[:, b % 2, c, t * P:(t + 1) * P], attended[:, b % 2, c, :], c,
                              c == 1)
                last.then_inc(xm_done, 1)

            def gt():
                pe.wait_ge(centred, 1)
                pe.wait_ge(ct_sb, 2)
                for c in range(HC):
                    last = turn(p_gt[:, c * E:(c + 1) * E], gate_sb[:, c * P:(c + 1) * P], E)
                last.then_inc(gt_done, 1)

            def rk(b):
                r = p_rank[:, 0:2 * E]
                if b == 0:
                    pe.wait_ge(q_sb, B)
                else:
                    pe.wait_ge(rank_read, b)
                    pe.wait_ge(mask_done, b)
                for n in range(2 * b):
                    nc.tensor.matmul(r, ones[:], mask[:, n // 2, n % 2:n % 2 + 1, :].to_broadcast([P, 2, E]),
                                     start=(n == 0), stop=False, skip_group_check=True)
                pe.wait_ge(mask_done, b + 1)
                nc.tensor.matmul(r, before[:], mask[:, b, :, :], start=(b == 0), stop=False, skip_group_check=True)
                nc.tensor.matmul(r[:, E:2 * E], ones[:], mask[:, b, 0, :], start=False, stop=True,
                                 skip_group_check=True).then_inc(rk_done, 1)

            def weightsT():
                pe.wait_ge(wqk_here, 32)
                for w in range(2):
                    last = turn(p_wT[:, w * C:(w + 1) * C], wqk[:, w, :])
                last.then_inc(wT_done, 1)
                keep_warm(WARM_INPUT)

            pe.wait_ge(ident_done, 1)
            keep_warm(WARM_START)
            ct(0)
            weightsT()
            q(0)
            k(0)
            ct(1)
            q(1)
            en(0)
            k(1)
            q(2)
            gt()
            tl(0)
            k(2)
            en(1)
            k(3)
            en(2)
            at(0)
            q(3)
            xm(0)
            at(1)
            xm(1)
            tl(1)
            en(3)
            at(2)
            xm(2)
            tl(2)
            rk(0)
            xm(3)
            xm(4)
            at(3)
            xm(5)
            tl(3)
            disp(0)
            rk(1)
            xm(6)
            xm(7)
            disp(1)
            disp(2)
            disp(3)
            rk(2)
            rk(3)
            disp(4)
            disp(5)
            disp(6)
            disp(7)

            def dT(i):
                pe.wait_ge(stok_done, i + 1)
                if i >= 2:
                    pe.wait_ge(dT_sb, i - 1)
                for c in range(HC):
                    last = turn(p_dT[i % 2][:, c * P:(c + 1) * P], stok[:, i % 2, c * P:(c + 1) * P])
                last.then_inc(dT_done, 1)

            def mm1(e, then=()):
                pe.wait_ge(wi_here[e], 16)
                if e == 0:
                    pe.wait_ge(disp_sb, 1)
                else:
                    pe.wait_ge(dT_sb, max(i for i in range(INS) if FIRST_USE[i] <= e) + 1)
                for j, (a, z_) in enumerate(GROUPS):
                    if e:
                        pe.wait_ge(gelu_done, NG * (e - 1) + j + 1)
                    for i in range(a, z_):
                        for c in range(HC):
                            last = mm(p_h[j][:, (i - a) * CAP:(i - a + 1) * CAP], wi_sb[:, e, c, i * P:(i + 1) * P],
                                      dispT[:, c, e, :], c, c == HC - 1)
                    last.then_inc(h_done, 1)
                    if j == 1:
                        for i in then:
                            dT(i)

            gelu_rows = [gelu[:, e % RING, :, :] for e in range(E)]

            def bank_free(n):
                if n >= 2:
                    pe.wait_ge(y_done, n - 1)

            def mm2(e, n, then=()):
                pe.wait_ge(wo_here[e], 16)
                bank_free(n)
                for j, (a, z_) in enumerate(GROUPS):
                    pe.wait_ge(gelu_done, NG * e + j + 1)
                    if j == 2:
                        for i in then:
                            dT(i)
                    for i in range(a, z_):
                        last = mm(p_o[n % 2][:, 0:H], gelu_rows[e][:, i, 0:P], wo_sb[:, e, i, :], i, i == IC - 1)
                last.then_inc(o_done, 1)

            def mm2_stack(r, n):
                bank_free(n)
                for i in range(IC):
                    for j in range(PER_STACK):
                        e = r * PER_STACK + j
                        last = mm(p_o[n % 2][j * REM:(j + 1) * REM, 0:H], gelu_rows[e][:, i, P:CAP],
                                  wo_sb[:, e, i, :], i, i == IC - 1)
                last.then_inc(o_done, 1)

            keep_warm(WARM_DISPATCH)
            outs = iter(range(OUTS))
            mm1(0)
            mm2(0, next(outs), then=INS_AT[0])
            mm1(1, then=INS_AT[1])
            for s in range(2, E + 1):
                for i in INS_AT[s]:
                    dT(i)
                if s < E:
                    mm1(s)
                mm2(s - 1, next(outs))
                if s % PER_STACK == 0:
                    mm2_stack(s // PER_STACK - 1, next(outs))


_INS = ["x", "ctx_1024", "L0_xattn_Wq", "L0_xattn_bq", "L0_xattn_Wk", "L0_xattn_bk", "L0_ffn_gate_weight",
        "L0_ffn_wi", "L0_ffn_wo"]


def kernel(**inputs):
    import numpy as _np
    import concourse.bacc as _bacc
    from concourse import mybir as _mybir
    from concourse.bass_utils import run_bass_kernel_spmd as _run

    nc = _bacc.Bacc("TRN2", target_bir_lowering=False, num_devices=1)
    arrays, args = {}, []
    for name in _INS:
        a = _np.ascontiguousarray(inputs[name])
        arrays[f"in_{name}"] = a
        args.append(nc.dram_tensor(f"in_{name}", a.shape, _mybir.dt.from_np(a.dtype), kind="ExternalInput").ap())
    args.append(nc.dram_tensor("out_0", (B, S, H), F32, kind="ExternalOutput").ap())
    xattn_moe(nc, *args)
    r = _run(nc, [arrays], core_ids=[0])
    return r.results[0]["out_0"]
```
